# Optimizing a Trainium2 kernel written in Bass

```python
import numpy as np
import jax
import jax.numpy as jnp

def _softmax(x, axis=-1):
    return jax.nn.softmax(x, axis=axis)

def _gelu(x):
    return jax.nn.gelu(x, approximate=True)

def _silu(x):
    return jax.nn.silu(x)

def _sigmoid(x):
    return jax.nn.sigmoid(x)

def _layernorm(x, axis=-1, eps=1e-05):
    m = jnp.mean(x, axis=axis, keepdims=True)
    v = jnp.var(x, axis=axis, keepdims=True)
    return (x - m) / jnp.sqrt(v + eps)

def _scatter_add(tgt, idx, src, axis=0):
    return tgt.at[idx].add(src)

def _segment_sum(src, seg, n):
    return jax.ops.segment_sum(src, seg, n)
kernel_name = 'mk_prb_d1_jaxref_r8_a59249'

def setup_inputs(seed: int=0):
    np.random.seed(seed)
    _w = jnp.asarray

    def _L0_attn_setup():
        import jax, jax.numpy as jnp
        import numpy as np
        B, S, HID = (2, 256, 128)
        H, DH = (16, 64)
        RAMP = 32
        NEG = -1000000000.0

        def _split_heads(x):
            b, s, _ = x.shape
            return x.reshape(b, s, H, DH).transpose(0, 2, 1, 3)
        key = jax.random.key(seed)
        ks = jax.random.split(key, 6)
        sc = 1.0 / np.sqrt(HID)
        return {'query': jax.random.normal(ks[0], (B, S, HID), dtype=jnp.float32), 'Wq': jax.random.normal(ks[1], (HID, H * DH), dtype=jnp.float32) * sc, 'Wk': jax.random.normal(ks[2], (HID, H * DH), dtype=jnp.float32) * sc, 'Wv': jax.random.normal(ks[3], (HID, H * DH), dtype=jnp.float32) * sc, 'Wo': jax.random.normal(ks[4], (H * DH, HID), dtype=jnp.float32) * sc, 'span_val': jax.random.uniform(ks[5], (1, H, 1, 1), dtype=jnp.float32, minval=0.0, maxval=0.2)}
    _L0_attn_in = _L0_attn_setup()

    def _L0_ffn_setup():
        import jax, jax.numpy as jnp
        import numpy as np
        B, S, D_IN, D_OUT = (16, 512, 128, 128)
        ACT_BITS = 8
        QB = float(2 ** (ACT_BITS - 1) - 1)
        key = jax.random.key(seed)
        k1, k2, k3 = jax.random.split(key, 3)
        x = jax.random.normal(k1, (B, S, D_IN), dtype=jnp.float32)
        ternary_weight = jax.random.randint(k2, (D_OUT, D_IN), 0, 3, dtype=jnp.int32)
        bias = jax.random.normal(k3, (D_OUT,), dtype=jnp.float32)
        act_scale = (jnp.max(jnp.abs(x)) / QB).astype(jnp.float32)
        return {'x': x, 'ternary_weight': ternary_weight, 'bias': bias, 'act_scale': act_scale}
    _L0_ffn_in = _L0_ffn_setup()
    _d = {'L0_attn_query': _L0_attn_in['query'], 'L0_attn_Wq': _L0_attn_in['Wq'], 'L0_attn_Wk': _L0_attn_in['Wk'], 'L0_attn_Wv': _L0_attn_in['Wv'], 'L0_attn_Wo': _L0_attn_in['Wo'], 'L0_attn_span_val': _L0_attn_in['span_val'], 'L0_ffn_ternary_weight': _L0_ffn_in['ternary_weight'], 'L0_ffn_bias': _L0_ffn_in['bias'], 'L0_ffn_act_scale': _L0_ffn_in['act_scale']}
    _x0 = _d['L0_attn_query']
    _d['L0_attn_query'] = jax.random.normal(jax.random.fold_in(jax.random.key(seed), 1), (4, 1024, 128), dtype=_x0.dtype)
    del _x0
    return _d

def reference(L0_attn_query, L0_attn_Wq, L0_attn_Wk, L0_attn_Wv, L0_attn_Wo, L0_attn_span_val, L0_ffn_ternary_weight, L0_ffn_bias, L0_ffn_act_scale):

    def _L0_attn_ref(query, Wq, Wk, Wv, Wo, span_val):
        import jax, jax.numpy as jnp
        import numpy as np
        B, S, HID = (2, 256, 128)
        H, DH = (16, 64)
        RAMP = 32
        NEG = -1000000000.0

        def _split_heads(x):
            b, s, _ = x.shape
            return x.reshape(b, s, H, DH).transpose(0, 2, 1, 3)
        q = _split_heads(query @ Wq)
        k = _split_heads(query @ Wk)
        v = _split_heads(query @ Wv)
        w = jnp.einsum('bhqd,bhkd->bhqk', q, k) / DH
        s = q.shape[2]
        causal = jnp.triu(jnp.full((s, s), NEG, dtype=w.dtype), k=1)
        w = w + causal[None, None]
        w = jax.nn.softmax(w, axis=-1)
        attn_span = jnp.float32(s)
        tmpl = jnp.arange(s, dtype=jnp.float32).reshape(1, 1, 1, s)
        mask = jnp.clip((tmpl + span_val * attn_span) / (RAMP + 1), 0.0, 1.0)
        w = w * mask
        w = w / (jnp.sum(w, axis=-1, keepdims=True) + 1e-08)
        out = jnp.einsum('bhqk,bhkd->bhqd', w, v)
        out = out.transpose(0, 2, 1, 3).reshape(out.shape[0], s, H * DH)
        return out @ Wo

    def _L0_ffn_ref(x, ternary_weight, bias, act_scale):
        import jax, jax.numpy as jnp
        import numpy as np
        B, S, D_IN, D_OUT = (16, 512, 128, 128)
        ACT_BITS = 8
        QB = float(2 ** (ACT_BITS - 1) - 1)
        scale = jnp.maximum(act_scale, 1e-05)
        x_int = jnp.clip(jnp.round(x / scale), -QB, QB)
        x_dq = jnp.nan_to_num(x_int * scale, nan=0.0, posinf=10000.0, neginf=-10000.0)
        w = ternary_weight.astype(jnp.float32) - 1.0
        return jnp.einsum('bsi,oi->bso', x_dq, w) + bias
    x = L0_attn_query
    xn = _layernorm(x, axis=-1)
    x = x + _L0_attn_ref(xn, L0_attn_Wq, L0_attn_Wk, L0_attn_Wv, L0_attn_Wo, L0_attn_span_val) + _L0_ffn_ref(xn, L0_ffn_ternary_weight, L0_ffn_bias, L0_ffn_act_scale)
    return x

_drawn_inputs = setup_inputs


def setup_inputs(seed=0):
    import zlib

    import numpy as np

    out = dict(_drawn_inputs(seed))
    spreads = {}
    factors = {'L0_attn_Wq': 8.0, 'L0_attn_Wk': 8.0, 'L0_attn_span_val': 64.0}
    for name, (base, spread) in spreads.items():
        noise = np.random.default_rng([zlib.crc32(name.encode()), seed]).standard_normal(out[name].shape)
        drawn = base * np.exp(spread * noise) if base else spread * noise
        out[name] = jnp.asarray(drawn.astype(out[name].dtype))
    for name, factor in factors.items():
        out[name] = (out[name] * factor).astype(out[name].dtype)
    return out
```

```python
from contextlib import ExitStack

import concourse.bass as bass
from concourse import mybir

ALU = mybir.AluOpType
ACT = mybir.ActivationFunctionType
AX = mybir.AxisListType.X
F32 = mybir.dt.float32
F32R = mybir.dt.float32r
BF16 = mybir.dt.bfloat16
I32 = mybir.dt.int32
U32 = mybir.dt.uint32

P = 128
HALF = 512
RAMP = 32
EPS_LN = 1e-5
EPS_SUM = 1e-8
ACT_QB = 127.0
ROUND = 12582912.0
FLT_MAX = 3.4028234663852886e38
MASKED = -1e30

MAX_UNITS = (
    [(0, 0, 128, (0, 1)), (1, 0, 256, (0, 1))]
    + [(j, 0, 128 * (j + 1), (h,)) for j in (2, 3) for h in (0, 1)]
    + [(j, 0, 512, (h,)) for j in (4, 5, 6, 7) for h in (0, 1)]
    + [(4, 512, 128, (0, 1)), (5, 512, 256, (0, 1))]
    + [(j, 512, 128 * (j - 3), (h,)) for j in (6, 7) for h in (0, 1)]
)
M = [f"M{n}" for n in range(len(MAX_UNITS))]

SLOTS = [
    ["Q0", "K0"],
    ["D1p"],
    M[0:3],
    ["Y1p"] + M[3:6],
    ["Q1", "K1"],
    M[6:8],
    ["D0", M[8]],
    M[9:12],
    ["F"] + M[12:16],
    M[16:20],
    ["T"],
    ["Y0", "V0", "V1"],
]
OF_PAIR_BEFORE = ("D1p", "Y1p")
OF_THIS_PAIR = ("D0", "Y0", "F")


def slots_of(first, last):
    return [
        [u for u in slot if not (first and u in OF_PAIR_BEFORE)
         and not (last and u not in OF_THIS_PAIR + OF_PAIR_BEFORE)]
        for slot in SLOTS
    ]


def flat(slots):
    return [u for slot in slots for u in slot]


TURNS = [f"X{n}" for n in range(8)]
PREP0 = [u for u in flat(SLOTS) if u not in OF_THIS_PAIR + OF_PAIR_BEFORE]
PROLOGUE = TURNS + PREP0 + ["W"]
STEADY = flat(slots_of(False, False))
FIRST = flat(slots_of(True, False))
LAST = flat(slots_of(False, True))


def ring_index(i, name, n_pairs):
    if isinstance(i, int) and i == 0:
        return len(PROLOGUE) + FIRST.index(name)
    before = len(PROLOGUE) + len(FIRST) - len(STEADY)
    if isinstance(i, int) and i == n_pairs - 1:
        return before + len(STEADY) * i + LAST.index(name)
    return i * len(STEADY) + (before + STEADY.index(name))


def attention_ffn(nc, x_dram, wq_dram, wk_dram, wv_dram, wo_dram, span_dram, tern_dram, bias_dram,
                  scale_dram, out_dram):
    B, S, D = x_dram.shape
    H = span_dram.shape[1]
    DH = wq_dram.shape[1] // H
    NPB = H // 2
    NP = B * NPB
    KB = S // P
    HB = HALF // P
    NB = B * KB
    TILES = [(0, kb) for kb in range(HB)] + [(1, kb) for kb in range(KB)]
    NT = len(TILES)
    NDIAG = sum(kb >= HB * c for c, kb in TILES)
    assert D == P and DH == 64 and S == 2 * HALF and NT == 12 and KB == 8 and NB == NP

    def first_col(t):
        c, kb = TILES[t]
        return max(0, kb - HB * c) * P

    def is_diag(t):
        c, kb = TILES[t]
        return kb >= HB * c

    diag_upto = [sum(is_diag(u) for u in range(t + 1)) for t in range(NT)]

    ctx = ExitStack()
    with ctx:
        def sb(name, shape, dt=F32):
            return ctx.enter_context(nc.sbuf_tensor(name, shape, dt))

        def sem(name):
            return ctx.enter_context(nc.semaphore(name))

        x_sb = sb("x_sb", [P, NB, D])
        xn_sb = sb("xn_sb", [P, NB, D])
        xnT = sb("xnT", [P, NB * P])
        xT_cur = sb("xT_cur", [P, S])
        wq_cur = sb("wq_cur", [P, P])
        wk_cur = sb("wk_cur", [P, P])
        wv_cur = sb("wv_cur", [P, P])
        wo_cur = sb("wo_cur", [P, P])
        q12 = [[sb(f"q12_{p}{h}", [P, S], F32R) for h in range(2)] for p in range(2)]
        q1m = [[sb(f"q1m_{p}{h}", [DH + 1, S], F32R) for h in range(2)] for p in range(2)]
        k11 = [[sb(f"k11_{p}{h}", [P, S], F32R) for h in range(2)] for p in range(2)]
        k2n = [[sb(f"k2n_{p}{h}", [DH + 1, S], F32R) for h in range(2)] for p in range(2)]
        v_sb = [sb(f"v_{p}", [P, KB, 2, DH]) for p in range(2)]
        NPROB = 4
        prob = [sb(f"prob_{n}", [P, 2, HALF]) for n in range(NPROB)]
        psumd = [sb(f"psumd_{c}", [P, 2, HALF]) for c in range(2)]
        rden = sb("rden", [P, HALF])
        o_sb = [sb(f"o_{c}", [P, HALF]) for c in range(2)]
        rowmax = [sb(f"rowmax_{p}", [P, 2, KB]) for p in range(2)]
        rowmax2 = [sb(f"rowmax2_{p}", [P, 2, HB]) for p in range(2)]
        maxrow = sb("maxrow", [2 * KB, P], F32R)
        tab_cur = [sb(f"tab_{p}", [P, 2, KB, 2]) for p in range(2)]
        ident = sb("ident", [P, P])
        ident_b = sb("ident_b", [P, P], BF16)
        causal_b = sb("causal_b", [P, P], BF16)
        ones = sb("ones", [P, DH])
        key_no = sb("key_no", [P, KB])
        span_b = sb("span_b", [P, H])
        mask = sb("mask", [P, NPB, KB, 2])
        wrec = sb("wrec", [P, NPB, KB, 2])
        wgt = sb("wgt", [P, NPB, KB, 2])
        table = sb("table", [P, NPB, 2, KB, 2])
        tern_i = sb("tern_i", [P, P], I32)
        tern = sb("tern", [P, P])
        ternT = sb("ternT", [P, P])
        bias_b = sb("bias_b", [P, P])
        scale_b = sb("scale_b", [P, 1])
        sc = sb("sc", [P, 8])
        fq = sb("fq", [P, P])
        over = sb("over", [P, 2, P], U32)
        big = sb("big", [P, 2, P])
        stats = sb("stats", [P, NB, 6])
        mv = sb("mv", [P, NB, 2])
        vpe = sb("vpe", [P, NB])
        std = sb("std", [P, NB])
        rstd = sb("rstd", [P, NB])
        tmp = sb("tmp", [P, NB])

        scores = ctx.enter_context(nc.psum_tensor("scores", [P, 2, 2, HALF], F32))
        ring = ctx.enter_context(nc.psum_tensor("ring", [P, 2, HALF], F32))
        pv = ctx.enter_context(nc.psum_tensor("pv", [P, 2, HALF], F32))

        x_landed = [sem(f"x_landed{b}") for b in range(B)]
        small_landed = sem("small_landed")
        wqkv_landed = sem("wqkv_landed")
        xT_landed = sem("xT_landed")
        wo_landed = sem("wo_landed")
        maxrow_landed = sem("maxrow_landed")
        out_stored = sem("out_stored")
        consts_done = sem("consts_done")
        pool_step = sem("pool_step")
        bias_added = sem("bias_added")
        tab_done = sem("tab_done")
        sel_done = sem("sel_done")
        acc_done = sem("acc_done")
        var_done = sem("var_done")
        std_done = sem("std_done")
        wgt_done = sem("wgt_done")
        ln_done = sem("ln_done")
        xn_done = sem("xn_done")
        dve_step = sem("dve_step")
        table_done = sem("table_done")
        tern_done = sem("tern_done")
        fq_step = sem("fq_step")
        scores_ready = sem("scores_ready")
        exp_done = sem("exp_done")
        pv_done = sem("pv_done")
        norm_done = sem("norm_done")
        hi_done = sem("hi_done")
        unit_ready = sem("unit_ready")
        unit_free = sem("unit_free")
        max_done = sem("max_done")
        apart = sem("apart")

        block = ctx.enter_context(nc.Block())

        NCONST = 11
        FQ_STEPS = 7
        XT_READY = 2

        def wait_apart(engine, sem, value):
            engine.wait_ge(sem, value)
            engine.sem_inc(apart, 1)

        def prologue_index(name):
            return PROLOGUE.index(name)

        def prep_index(i, name):
            if isinstance(i, int) and i == 0:
                return prologue_index(name)
            return ring_index(i - 1, name, NP)

        @block.sync
        def _(sp):
            for b in range(B):
                sp.dma_start(x_sb[:, b * KB:(b + 1) * KB, :],
                             x_dram[b, :, :].rearrange("(n p) d -> p n d", p=P)).then_inc(x_landed[b], 16)

            def load_qkv(i):
                hp = i % NPB
                b = i // NPB
                for w, dst in ((wq_dram, wq_cur), (wk_dram, wk_cur), (wv_dram, wv_cur)):
                    sp.dma_start(dst[:, :], w[:, bass.ds(hp * P, P)]).then_inc(wqkv_landed, 16)
                sp.dma_start(xT_cur[:, :], xnT[:, bass.ds(b * S, S)]).then_inc(xT_landed, 16)

            def load_wo(i):
                sp.dma_start(wo_cur[:, :], wo_dram[bass.ds((i % NPB) * P, P), :]).then_inc(wo_landed, 16)

            def place_maxrow(i, p):
                sp.wait_ge(unit_free, prep_index(i, "T") + 1)
                for h in range(2):
                    sp.dma_start(q1m[p][h][DH:DH + 1, :].bitcast(F32),
                                 maxrow[h * KB:(h + 1) * KB, :].bitcast(F32)).then_inc(maxrow_landed, 16)

            sp.wait_ge(unit_free, XT_READY)
            load_qkv(0)
            load_wo(0)
            place_maxrow(0, 0)
            sp.wait_ge(unit_ready, prologue_index("V1") + 1)
            sp.wait_ge(unit_free, len(TURNS))
            load_qkv(1)
            place_maxrow(1, 1)
            sp.wait_ge(unit_ready, ring_index(0, "V1", NP) + 1)
            load_qkv(2)

            def pair(i, p, last=False):
                sp.wait_ge(unit_ready, ring_index(i, "Y1p", NP) + 1)
                load_wo(i)
                if not last:
                    place_maxrow(i + 1, 1 - p)
                    sp.wait_ge(unit_ready, ring_index(i, "V1", NP) + 1)
                    load_qkv(i + 2)

            with sp.Fori(0, (NP - 2) // 2 - 1) as j:
                pair(2 * j + 1, 1)
                pair(2 * j + 2, 0)
            pair(NP - 3, 1)
            pair_i = NP - 2
            sp.wait_ge(unit_ready, ring_index(pair_i, "Y1p", NP) + 1)
            load_wo(pair_i)
            place_maxrow(NP - 1, 1)
            pair(NP - 1, 1, last=True)
            sp.wait_ge(unit_free, ring_index(NP - 1, "Y0", NP) + 3)
            for b in range(B):
                sp.dma_start(out_dram[b, :, :].rearrange("(n p) d -> p n d", p=P),
                             x_sb[:, b * KB:(b + 1) * KB, :]).then_inc(out_stored, 16)
            sp.wait_ge(out_stored, 16 * B)

        @block.gpsimd
        def _(pool):
            g = nc.gpsimd
            g.memset(ident[:, :], 0.0).then_inc(pool_step, 1)
            g.memset(ident_b[:, :], 0.0).then_inc(pool_step, 1)
            g.memset(causal_b[:, :], 0.0).then_inc(pool_step, 1)
            g.memset(ones[:, :], 1.0).then_inc(consts_done, 1)
            g.memset(big[:, 0, :], 1e4).then_inc(consts_done, 1)
            g.memset(big[:, 1, :], -1e4).then_inc(consts_done, 1)
            g.iota(key_no[:, :], [[P, KB]], base=0, channel_multiplier=1,
                   allow_small_or_imprecise_dtypes=True).then_inc(consts_done, 1)
            pool.wait_ge(pool_step, 3)
            g.affine_select(out=ident[:, :], in_=ident[:, :], compare_op=ALU.not_equal, fill=1.0,
                            base=0, pattern=[[-1, P]], channel_multiplier=1).then_inc(consts_done, 1)
            g.affine_select(out=ident_b[:, :], in_=ident_b[:, :], compare_op=ALU.not_equal, fill=1.0,
                            base=0, pattern=[[-1, P]], channel_multiplier=1).then_inc(consts_done, 1)
            g.affine_select(out=causal_b[:, :], in_=causal_b[:, :], compare_op=ALU.is_ge, fill=MASKED,
                            base=0, pattern=[[-1, P]], channel_multiplier=1).then_inc(consts_done, 1)
            pool.wait_ge(xn_done, NB)
            pool.wait_ge(small_landed, 64)
            g.tensor_tensor(x_sb[:, :, :], x_sb[:, :, :], bias_b[:, :].unsqueeze(1).to_broadcast([P, NB, P]),
                            ALU.add).then_inc(bias_added, 1)

            def pair_table(i, p):
                g.tensor_copy(tab_cur[p][:, :, :, :],
                              table[:, bass.ds(i % NPB, 1), :, :, :].rearrange("p o a k h -> p (o a) k h")
                              ).then_inc(tab_done, 1)

            pool.wait_ge(table_done, 1)
            pair_table(0, 0)

            def pair(i, p, last=False):
                if not last:
                    pair_table(i + 1, 1 - p)
                for t in range(NT):
                    c, kb = TILES[t]
                    lo = first_col(t)
                    pr = prob[t % NPROB]
                    if kb == 0 and not (isinstance(i, int) and i == 0):
                        pool.wait_ge(unit_ready, (ring_index(i - 1, "D0", NP) if c == 0
                                                  else ring_index(i, "D1p", NP)) + 1)
                    if is_diag(t):
                        wait_apart(pool, exp_done, i * NT + (t + 1))
                    else:
                        pool.wait_ge(exp_done, i * NT + (t + 1))
                    if is_diag(t):
                        d = pr[:, :, lo:lo + P]
                        g.affine_select(out=d, in_=d, compare_op=ALU.is_ge, fill=0.0, base=0,
                                        pattern=[[0, 2], [1, P]], channel_multiplier=-1).then_inc(sel_done, 1)
                        if t == 0:
                            wait_apart(pool, sel_done, i * NDIAG + 1)
                        else:
                            pool.wait_ge(sel_done, i * NDIAG + diag_upto[t])
                    acc = psumd[c]
                    if kb == 0:
                        if c == 0:
                            g.tensor_scalar(acc[:, :, 0:P], pr[:, :, 0:P], 1.0, None, ALU.mult)
                    elif kb == 1:
                        g.tensor_tensor(acc[:, :, lo:HALF], prob[(t - 1) % NPROB][:, :, lo:HALF],
                                        pr[:, :, lo:HALF], ALU.add).then_inc(acc_done, 2)
                    else:
                        pool.wait_ge(acc_done, i * NT + t)
                        g.tensor_tensor(acc[:, :, lo:HALF], acc[:, :, lo:HALF], pr[:, :, lo:HALF],
                                        ALU.add).then_inc(acc_done, 1)

            pair(0, 0)
            with pool.Fori(0, (NP - 2) // 2) as j:
                pair(2 * j + 1, 1)
                pair(2 * j + 2, 0)
            pair(NP - 1, 1, last=True)

        @block.scalar
        def _(act):
            a = nc.scalar
            for dst, src in ((span_b[:, :], span_dram.rearrange("a h b c -> (a b c) h").to_broadcast([P, H])),
                             (bias_b[:, :], bias_dram.unsqueeze(0).to_broadcast([P, P])),
                             (scale_b[:, :], scale_dram.to_broadcast([P, 1])),
                             (tern_i[:, :], tern_dram[:, :])):
                act.dma_start(dst, src).then_inc(small_landed, 16)
            act.wait_ge(var_done, 1)
            a.activation(std[:, :], vpe[:, :], ACT.Sqrt).then_inc(std_done, 1)
            act.wait_ge(wgt_done, 1)
            a.activation(table[:, :, 0, :, :], wgt[:, :, :, :], ACT.Ln).then_inc(ln_done, 1)

            def exps(i, p, t):
                lo = first_col(t)
                act.wait_ge(scores_ready, i * NT + (t + 1))
                if not (isinstance(i, int) and i == 0 and t < NPROB):
                    act.wait_ge(pv_done, i * NT + (t - NPROB + 1))
                    act.wait_ge(acc_done, i * NT + (t - NPROB + 1))
                if t == 0:
                    act.wait_ge(tab_done, i + 1)
                kb = TILES[t][1]
                for h in range(2):
                    last = a.activation(prob[t % NPROB][:, h, lo:HALF], scores[:, t % 2, h, lo:HALF],
                                        ACT.Exp, bias=tab_cur[p][:, 0, kb, h:h + 1], scale=1.0 / DH)
                last.then_inc(exp_done, 1)

            def high_parts(i, p, name):
                act.wait_ge(unit_ready, prep_index(i, name) + 1)
                r = prep_parity[name]
                cols = slice(int(name[1]) * HALF, (int(name[1]) + 1) * HALF)
                for h in range(2):
                    src = ring[h * DH:(h + 1) * DH, r, :]
                    if name[0] == "Q":
                        a.activation(q1m[p][h][0:DH, cols], src, ACT.Copy)
                        last = a.activation(q12[p][h][0:DH, cols], src, ACT.Copy)
                    else:
                        a.activation(k11[p][h][0:DH, cols], src, ACT.Copy)
                        last = a.activation(k11[p][h][DH:P, cols], src, ACT.Copy)
                last.then_inc(hi_done, 1)

            prep_parity = {u: prologue_index(u) % 2 for u in PREP0}
            for u in PREP0:
                if u[0] in "QK":
                    high_parts(0, 0, u)

            def pair(i, p, first=False, last=False):
                slots = slots_of(first, last)
                order = flat(slots)
                base = len(PROLOGUE) if first else len(PROLOGUE) + len(FIRST) - len(STEADY)
                prep_parity.update({u: (base + n) % 2 for n, u in enumerate(order)})
                exps(i, p, 0)
                for s in range(NT):
                    if s + 1 < NT:
                        exps(i, p, s + 1)
                    for u in slots[s]:
                        if u[0] in "QK":
                            high_parts(i + 1, 1 - p, u)

            pair(0, 0, first=True)
            with act.Fori(0, (NP - 2) // 2) as j:
                pair(2 * j + 1, 1)
                pair(2 * j + 2, 0)
            pair(NP - 1, 1, last=True)

        @block.vector
        def _(dve):
            v = nc.vector
            steps = [0]

            def then(ins):
                steps[0] += 1
                ins.then_inc(dve_step, 1)
                dve.wait_ge(dve_step, steps[0])

            for p in range(2):
                for h in range(2):
                    v.memset(k2n[p][h][DH:DH + 1, :].bitcast(F32), -1.0).then_inc(consts_done, 1)
            for b in range(B):
                dve.wait_ge(x_landed[b], 16)
                for n in range(b * KB, (b + 1) * KB):
                    last = v.bn_stats(stats[:, n, :], x_sb[:, n, :])
            then(last)
            for n in range(NB):
                last = v.bn_aggr(mv[:, n, :], stats[:, n, :])
            then(last)
            v.tensor_scalar(vpe[:, :], mv[:, :, 1], EPS_LN, None, ALU.add).then_inc(var_done, 1)
            dve.wait_ge(consts_done, NCONST)
            dve.wait_ge(small_landed, 64)
            then(v.tensor_scalar(span_b[:, :], span_b[:, :], float(S), None, ALU.mult))
            for h in range(H):
                last = v.tensor_scalar(mask[:, h // 2, :, h % 2], key_no[:, :], span_b[:, h:h + 1],
                                       1.0 / (RAMP + 1), ALU.add, ALU.mult)
            then(last)
            then(v.tensor_scalar(mask[:, :, :, :], mask[:, :, :, :], 0.0, 1.0, ALU.max, ALU.min))
            v.tensor_scalar(wgt[:, :, :, :], mask[:, :, :, :], EPS_SUM, None, ALU.add).then_inc(wgt_done, 1)
            dve.wait_ge(std_done, 1)
            then(v.reciprocal(rstd[:, :], std[:, :]))
            then(v.tensor_tensor(tmp[:, :], rstd[:, :], rstd[:, :], ALU.mult))
            then(v.tensor_tensor(tmp[:, :], tmp[:, :], vpe[:, :], ALU.mult))
            then(v.tensor_scalar(tmp[:, :], tmp[:, :], -0.5, 1.5, ALU.mult, ALU.add))
            then(v.tensor_tensor(rstd[:, :], rstd[:, :], tmp[:, :], ALU.mult))

            def normalise(b):
                for n in range(b * KB, (b + 1) * KB):
                    v.tensor_scalar(xn_sb[:, n, :], x_sb[:, n, :], mv[:, n, 0:1], rstd[:, n:n + 1],
                                    ALU.subtract, ALU.mult).then_inc(xn_done, 1)

            def turned(n):
                dve.wait_ge(unit_ready, n + 1)
                v.tensor_copy(xnT[:, n * HALF:(n + 1) * HALF], ring[:, n % 2, :]).then_inc(unit_free, 1)

            for b in range(B):
                normalise(b)
                if b == 0:
                    dve.wait_ge(wgt_done, 1)
                    then(v.reciprocal(wrec[:, :, :, :], wgt[:, :, :, :]))
                    dve.wait_ge(ln_done, 1)
                    v.tensor_tensor(table[:, :, 1, :, :], mask[:, :, :, :], wrec[:, :, :, :],
                                    ALU.mult).then_inc(table_done, 1)
                for n in (2 * b, 2 * b + 1):
                    turned(n)
            then(v.tensor_scalar(sc[:, 0:1], scale_b[:, :], 1e-5, None, ALU.max))
            v.memset(sc[:, 2:3], 0.0)
            v.memset(sc[:, 3:4], 1.0)
            then(v.tensor_scalar(sc[:, 4:5].bitcast(U32), scale_b[:, :], FLT_MAX, None, ALU.is_le))
            v.copy_predicated(sc[:, 2:3], sc[:, 4:5].bitcast(U32), sc[:, 0:1])
            then(v.copy_predicated(sc[:, 3:4], sc[:, 4:5].bitcast(U32), sc[:, 0:1]))
            then(v.reciprocal(sc[:, 5:6], sc[:, 3:4]))
            v.tensor_scalar(tern[:, :], tern_i[:, :], -1.0, None, ALU.add).then_inc(tern_done, 1)

            def fence(i, name):
                dve.wait_ge(unit_free, index(i, name) + 1)

            def index(i, name):
                return ring_index(i, name, NP)

            def low_parts(p, name, r):
                cols = slice(int(name[1]) * HALF, (int(name[1]) + 1) * HALF)
                for h in range(2):
                    src = ring[h * DH:(h + 1) * DH, r, :]
                    if name[0] == "Q":
                        last = v.tensor_tensor(q12[p][h][DH:P, cols], src,
                                               q1m[p][h][0:DH, cols].bitcast(F32), ALU.subtract)
                    else:
                        last = v.tensor_tensor(k2n[p][h][0:DH, cols], src,
                                               k11[p][h][0:DH, cols].bitcast(F32), ALU.subtract)
                last.then_inc(unit_free, 1)

            def prep_unit(i, p, name, r):
                if name[0] in "QK":
                    at = ["Q0", "K0", "Q1", "K1"].index(name)
                    dve.wait_ge(hi_done, i * 4 + (at + 1))
                    low_parts(p, name, r)
                    return
                dve.wait_ge(unit_ready, prep_index(i, name) + 1)
                if name[0] == "M":
                    j, k0, n, heads = MAX_UNITS[int(name[1:])]
                    dst = rowmax[p][:, :, j] if k0 == 0 else rowmax2[p][:, :, j - HB]
                    v.tensor_reduce(dst[:, heads[0]:heads[-1] + 1],
                                    ring[:, r, 0:n * len(heads)].rearrange("p (h k) -> p h k", k=n),
                                    axis=AX, op=ALU.max).then_inc(unit_free, 1)
                    if name == M[-1]:
                        fence_prep(i, name)
                        v.tensor_tensor(rowmax[p][:, :, HB:KB], rowmax[p][:, :, HB:KB],
                                        rowmax2[p][:, :, :], ALU.max).then_inc(max_done, 1)
                elif name == "T":
                    v.tensor_copy(maxrow[:, :], ring[0:2 * KB, r, 0:P]).then_inc(unit_free, 1)
                else:
                    if name == "V0":
                        dve.wait_ge(tab_done, i + 1)
                    b0 = HB * int(name[1])
                    v.tensor_tensor(v_sb[p][:, b0:b0 + HB, :, :],
                                    ring[:, r, :].rearrange("p (k h d) -> p k h d", k=HB, h=2),
                                    tab_cur[p][:, 1, b0:b0 + HB, :].unsqueeze(3).to_broadcast([P, HB, 2, DH]),
                                    ALU.mult).then_inc(unit_free, 1)

            def fence_prep(i, name):
                dve.wait_ge(unit_free, prep_index(i, name) + 1)

            for u in PREP0:
                prep_unit(0, 0, u, prologue_index(u) % 2)
            dve.wait_ge(unit_ready, prologue_index("W") + 1)
            v.tensor_copy(ternT[:, :], ring[:, prologue_index("W") % 2, 0:P]).then_inc(unit_free, 1)
            dve.wait_ge(bias_added, 1)

            def quantise(i):
                done = [0]

                def step(ins):
                    done[0] += 1
                    ins.then_inc(fq_step, 1)
                    if FQ_STEPS - 2 <= done[0] < FQ_STEPS:
                        wait_apart(dve, fq_step, i * FQ_STEPS + done[0])
                    elif done[0] < FQ_STEPS:
                        dve.wait_ge(fq_step, i * FQ_STEPS + done[0])

                step(v.tensor_scalar(fq[:, :], xnT[:, bass.ds(i * P, P)], sc[:, 5:6], ACT_QB, ALU.mult, ALU.min))
                step(v.tensor_scalar(fq[:, :], fq[:, :], -ACT_QB, ROUND, ALU.max, ALU.add))
                step(v.tensor_scalar(fq[:, :], fq[:, :], -ROUND, sc[:, 2:3], ALU.add, ALU.mult))
                step(v.tensor_scalar(over[:, 0, :], fq[:, :], FLT_MAX, None, ALU.is_gt))
                step(v.tensor_scalar(over[:, 1, :], fq[:, :], -FLT_MAX, None, ALU.is_lt))
                step(v.copy_predicated(fq[:, :], over[:, 0, :], big[:, 0, :]))
                step(v.copy_predicated(fq[:, :], over[:, 1, :], big[:, 1, :]))

            def own_unit(i, name, r):
                dve.wait_ge(unit_ready, index(i, name) + 1)
                c = 0 if name.endswith("0") else 1
                own = i if c == 0 else i - 1
                if name[0] == "D":
                    v.reciprocal(rden[:, :], ring[:, r, :]).then_inc(unit_free, 1)
                    fence(i, name)
                    v.tensor_tensor(o_sb[c][:, :], pv[:, c, :], rden[:, :], ALU.mult).then_inc(norm_done, 1)
                elif name[0] == "Y":
                    rows = x_sb[:, bass.ds((own // NPB) * KB + c * HB, HB), :]
                    v.tensor_tensor(rows, rows, ring[:, r, :].rearrange("p (n d) -> p n d", n=HB),
                                    ALU.add).then_inc(unit_free, 1)
                else:
                    rows = x_sb[:, bass.ds(i, 1), :]
                    v.tensor_tensor(rows, rows, ring[:, r, 0:P].unsqueeze(1), ALU.add).then_inc(unit_free, 1)

            def pair(i, p, first=False, last=False):
                slots = slots_of(first, last)
                at = len(PROLOGUE) if first else len(PROLOGUE) + len(FIRST) - len(STEADY)
                for s in range(NT):
                    for u in slots[s]:
                        r = at % 2
                        at += 1
                        if u in OF_THIS_PAIR or u in OF_PAIR_BEFORE:
                            if u == "F":
                                quantise(i)
                            own_unit(i, u, r)
                        else:
                            prep_unit(i + 1, 1 - p, u, r)
                return at % 2

            pair(0, 0, first=True)
            with dve.Fori(0, (NP - 2) // 2) as j:
                pair(2 * j + 1, 1)
                pair(2 * j + 2, 0)
            r = pair(NP - 1, 1, last=True)
            tail = index(NP - 1, "Y0") + 1
            dve.wait_ge(unit_ready, tail + 1)
            v.reciprocal(rden[:, :], ring[:, r, :]).then_inc(unit_free, 1)
            dve.wait_ge(unit_free, tail + 1)
            v.tensor_tensor(o_sb[1][:, :], pv[:, 1, :], rden[:, :], ALU.mult).then_inc(norm_done, 1)
            dve.wait_ge(unit_ready, tail + 2)
            rows = x_sb[:, (B - 1) * KB + HB:NB, :]
            v.tensor_tensor(rows, rows, ring[:, 1 - r, :].rearrange("p (n d) -> p n d", n=HB),
                            ALU.add).then_inc(unit_free, 1)

        @block.tensor
        def _(pe):
            t_ = nc.tensor
            pe.wait_ge(consts_done, NCONST)

            def begin_unit(n, r):
                if not isinstance(n, int) or n >= 2:
                    pe.wait_ge(unit_free, n - 1)

            for n in range(len(TURNS)):
                begin_unit(n, n % 2)
                pe.wait_ge(xn_done, HB * (n + 1))
                for k in range(HB):
                    last = t_.transpose(ring[:, n % 2, k * P:(k + 1) * P], xn_sb[:, n * HB + k, :], ident[:, :])
                last.then_inc(unit_ready, 1)

            def prep_unit(i, p, name, n, r):
                begin_unit(n, r)
                if name == "Q0":
                    pe.wait_ge(wqkv_landed, (i + 1) * 48)
                    pe.wait_ge(xT_landed, (i + 1) * 16)
                if name[0] in "QK":
                    c = int(name[1])
                    w = wq_cur if name[0] == "Q" else wk_cur
                    last = t_.matmul(ring[:, r, :], w[:, :], xT_cur[:, c * HALF:(c + 1) * HALF],
                                     start=True, stop=True)
                elif name[0] == "V":
                    for k in range(HB):
                        kb = HB * int(name[1]) + k
                        last = t_.matmul(ring[:, r, k * P:(k + 1) * P], xT_cur[:, kb * P:(kb + 1) * P],
                                         wv_cur[:, :], start=True, stop=True)
                elif name[0] == "M":
                    need = {M[0]: "K0", M[6]: "Q1", M[14]: "K1"}.get(name)
                    if need:
                        pe.wait_ge(unit_free, prep_index(i, need) + 1)
                    j, k0, w, heads = MAX_UNITS[int(name[1:])]
                    for at, h in enumerate(heads):
                        out = ring[:, r, at * w:(at + 1) * w]
                        diag = k0 + w == (j + 1) * P
                        last = t_.matmul(out, q12[p][h][:, j * P:(j + 1) * P], k11[p][h][:, k0:k0 + w],
                                         start=True, stop=not diag)
                        if diag:
                            last = t_.matmul(ring[:, r, (at + 1) * w - P:(at + 1) * w], ident_b[:, :],
                                             causal_b[:, :], start=False, stop=True)
                else:
                    pe.wait_ge(max_done, i + 1)
                    last = t_.matmul(ring[0:2 * KB, r, 0:P], rowmax[p][:, :, :].rearrange("p h j -> p (h j)"),
                                     ident[:, :], start=True, stop=True)
                last.then_inc(unit_ready, 1)

            for u in PREP0:
                n = prologue_index(u)
                prep_unit(0, 0, u, n, n % 2)
            n = prologue_index("W")
            begin_unit(n, n % 2)
            pe.wait_ge(tern_done, 1)
            t_.transpose(ring[:, n % 2, 0:P], tern[:, :], ident[:, :]).then_inc(unit_ready, 1)

            def denominators(i, c, r):
                pe.wait_ge(acc_done, i * NT + (HB if c == 0 else NT))
                for h in range(2):
                    last = t_.matmul(ring[h * DH:(h + 1) * DH, r, :], ones[:, :], psumd[c][:, h, :],
                                     start=True, stop=True)
                last.then_inc(unit_ready, 1)

            def output_projection(i, c, r):
                pe.wait_ge(norm_done, i * 2 + (c + 1))
                pe.wait_ge(wo_landed, (i + 1) * 16)
                for k in range(HB):
                    last = t_.matmul(ring[:, r, k * P:(k + 1) * P], o_sb[c][:, k * P:(k + 1) * P],
                                     wo_cur[:, :], start=True, stop=True)
                last.then_inc(unit_ready, 1)

            def own_unit(i, name, n, r):
                begin_unit(n, r)
                if name == "D0":
                    denominators(i, 0, r)
                elif name == "D1p":
                    denominators(i - 1, 1, r)
                elif name == "Y0":
                    output_projection(i, 0, r)
                elif name == "Y1p":
                    output_projection(i - 1, 1, r)
                else:
                    pe.wait_ge(fq_step, (i + 1) * FQ_STEPS)
                    t_.matmul(ring[:, r, 0:P], fq[:, :], ternT[:, :], start=True, stop=True
                              ).then_inc(unit_ready, 1)

            def scores_of(i, p, t):
                c, kb = TILES[t]
                lo = first_col(t)
                cols = slice(c * HALF + lo, (c + 1) * HALF)
                if not (isinstance(i, int) and i == 0 and t < 2):
                    pe.wait_ge(exp_done, i * NT + (t - 1))
                if t == 0:
                    pe.wait_ge(maxrow_landed, (i + 1) * 32)
                for h in range(2):
                    out = scores[:, t % 2, h, lo:HALF]
                    keys = slice(kb * P, (kb + 1) * P)
                    t_.matmul(out, k11[p][h][:, keys], q12[p][h][:, cols], start=True, stop=False)
                    last = t_.matmul(out, k2n[p][h][:, keys], q1m[p][h][:, cols], start=False, stop=True)
                last.then_inc(scores_ready, 1)

            def pv_of(i, p, t):
                c, kb = TILES[t]
                lo = first_col(t)
                if is_diag(t):
                    pe.wait_ge(sel_done, i * NDIAG + diag_upto[t])
                else:
                    pe.wait_ge(exp_done, i * NT + (t + 1))
                if kb == 0 and not (isinstance(i, int) and i == 0):
                    pe.wait_ge(norm_done, i * 2 + (c - 1))
                if t == 0:
                    pe.wait_ge(unit_free, prep_index(i, "V1") + 1)
                for h in range(2):
                    last = t_.matmul(pv[h * DH:(h + 1) * DH, c, lo:HALF], v_sb[p][:, kb, h, :],
                                     prob[t % NPROB][:, h, lo:HALF], start=(kb == 0),
                                     stop=(kb == HB * (c + 1) - 1))
                last.then_inc(pv_done, 1)

            def pair(i, p, first=False, last=False):
                slots = slots_of(first, last)
                base = len(PROLOGUE) if first else len(PROLOGUE) + len(FIRST) - len(STEADY)
                at = 0
                scores_of(i, p, 0)
                for s in range(NT):
                    if s + 1 < NT:
                        scores_of(i, p, s + 1)
                    for u in slots[s]:
                        n = i * len(STEADY) + (base + at) if not first else base + at
                        r = (base + at) % 2
                        at += 1
                        if u in OF_THIS_PAIR or u in OF_PAIR_BEFORE:
                            own_unit(i, u, n, r)
                        else:
                            prep_unit(i + 1, 1 - p, u, n, r)
                    pv_of(i, p, s)
                return (base + at) % 2

            pair(0, 0, first=True)
            with pe.Fori(0, (NP - 2) // 2) as j:
                pair(2 * j + 1, 1)
                pair(2 * j + 2, 0)
            r = pair(NP - 1, 1, last=True)
            tail = ring_index(NP - 1, "Y0", NP) + 1
            begin_unit(tail, r)
            denominators(NP - 1, 1, r)
            begin_unit(tail + 1, 1 - r)
            output_projection(NP - 1, 1, 1 - r)


_INS = ["L0_attn_query", "L0_attn_Wq", "L0_attn_Wk", "L0_attn_Wv", "L0_attn_Wo", "L0_attn_span_val",
        "L0_ffn_ternary_weight", "L0_ffn_bias", "L0_ffn_act_scale"]


def kernel(**inputs):
    import concourse.bacc as bacc
    import numpy as np
    from concourse.bass_utils import run_bass_kernel_spmd

    nc = bacc.Bacc("TRN2", target_bir_lowering=False, num_devices=1)
    arrays, args = {}, []
    for name in _INS:
        a = np.ascontiguousarray(inputs[name])
        if a.ndim == 0:
            a = a.reshape(1, 1)
        arrays[f"in_{name}"] = a
        args.append(nc.dram_tensor(f"in_{name}", a.shape, mybir.dt.from_np(a.dtype), kind="ExternalInput").ap())
    shape = inputs["L0_attn_query"].shape
    args.append(nc.dram_tensor("out_0", shape, F32, kind="ExternalOutput").ap())
    attention_ffn(nc, *args)
    r = run_bass_kernel_spmd(nc, [arrays], core_ids=[0])
    return r.results[0]["out_0"]
```

```python
from contextlib import ExitStack

import concourse.bass as bass
from concourse import mybir

ALU = mybir.AluOpType
ACT = mybir.ActivationFunctionType
AX = mybir.AxisListType.X
F32 = mybir.dt.float32
F32R = mybir.dt.float32r
BF16 = mybir.dt.bfloat16
I32 = mybir.dt.int32
U32 = mybir.dt.uint32

P = 128
HALF = 512
RAMP = 32
EPS_LN = 1e-5
EPS_SUM = 1e-8
ACT_QB = 127.0
ROUND = 12582912.0
FLT_MAX = 3.4028234663852886e38
MASKED = -1e30

MAX_UNITS = (
    [(0, 0, 128, (0, 1)), (1, 0, 256, (0, 1))]
    + [(j, 0, 128 * (j + 1), (h,)) for j in (2, 3) for h in (0, 1)]
    + [(j, 0, 512, (h,)) for j in (4, 5, 6, 7) for h in (0, 1)]
    + [(4, 512, 128, (0, 1)), (5, 512, 256, (0, 1))]
    + [(j, 512, 128 * (j - 3), (h,)) for j in (6, 7) for h in (0, 1)]
)
M = [f"M{n}" for n in range(len(MAX_UNITS))]

PE_LEAD = ["Q0", "K0"]
PE_PLAN = [
    [["D1p"], [], []],
    [[], [M[0]], []],
    [[M[1]], ["Q1"], [M[2]]],
    [[M[3]], [M[4]], ["Y1p"]],
    [[M[5]], ["K1"], [M[6]]],
    [[M[7]], [M[8]], ["V0"]],
    [[M[9]], ["D0"], [M[10]]],
    [[M[11]], [M[12]], ["V1"]],
    [[M[13]], [M[14]], [M[15]]],
    [[M[16]], [M[17]], ["F", M[18]]],
    [[M[19]], [], ["T"]],
    [["Y0"], [], []],
]
DVE_PLAN = (
    ["Q0", "q1", "K0", "q2", M[0], "q3", M[1], "D1p", "q4", M[2], M[3], "Q1", "q5", M[4], "Y1p", "q6", M[5]]
    + ["K1", "q7"] + M[6:9] + ["V0"] + M[9:11] + ["D0"] + M[11:13] + ["V1"] + M[13:18] + ["F"] + M[18:20]
    + ["T", "Y0"]
)
ACT_PLAN = ["P1p", "Q0", "e0", "K0", "e1", "D1p", "e2", "e3", "Q1", "P0", "e4", "e5", "K1", "e6", "e7", "D0",
            "e8", "e9", "e10", "e11"]
OF_PAIR_BEFORE = ("D1p", "Y1p", "P1p")
OF_THIS_PAIR = ("D0", "Y0", "F", "P0") + tuple(f"q{n}" for n in range(1, 8)) + tuple(f"e{n}" for n in range(12))


def kept(units, first, last):
    return [u for u in units if not (first and u in OF_PAIR_BEFORE)
            and not (last and u not in OF_THIS_PAIR + OF_PAIR_BEFORE)]


def of_prep(units):
    return [u for u in units if u not in OF_THIS_PAIR + OF_PAIR_BEFORE]


def ring_of(name):
    return "M" if name[0] == "M" else "A"


def in_ring(ring, units):
    return [u for u in units if ring_of(u) == ring]


PE_ORDER = PE_LEAD + [u for slot in PE_PLAN for place in slot for u in place]
TURNS = [f"X{n}" for n in range(8)]
PROLOGUE = {r: in_ring(r, TURNS + of_prep(PE_ORDER) + ["W"]) for r in "AM"}
STEADY = {r: in_ring(r, PE_ORDER) for r in "AM"}
FIRST = {r: in_ring(r, kept(PE_ORDER, True, False)) for r in "AM"}
LAST = {r: in_ring(r, kept(PE_ORDER, False, True)) for r in "AM"}
assert all(len(units[r]) % 2 == 0 for units in (PROLOGUE, STEADY, FIRST) for r in "AM")


def ring_index(i, name, n_pairs):
    r = ring_of(name)
    if isinstance(i, int) and i == 0:
        return len(PROLOGUE[r]) + FIRST[r].index(name)
    before = len(PROLOGUE[r]) + len(FIRST[r]) - len(STEADY[r])
    if isinstance(i, int) and i == n_pairs - 1:
        return before + len(STEADY[r]) * i + LAST[r].index(name)
    return i * len(STEADY[r]) + (before + STEADY[r].index(name))


def bank(name, where):
    return where[ring_of(name)].index(name) % 2


def attention_ffn(nc, x_dram, wq_dram, wk_dram, wv_dram, wo_dram, span_dram, tern_dram, bias_dram,
                  scale_dram, out_dram):
    B, S, D = x_dram.shape
    H = span_dram.shape[1]
    DH = wq_dram.shape[1] // H
    NPB = H // 2
    NP = B * NPB
    KB = S // P
    HB = HALF // P
    NB = B * KB
    TILES = [(0, kb) for kb in range(HB)] + [(1, kb) for kb in range(KB)]
    NT = len(TILES)
    assert D == P and DH == 64 and S == 2 * HALF and NT == 12 and KB == 8 and NB == NP

    def first_col(t):
        c, kb = TILES[t]
        return max(0, kb - HB * c) * P

    def is_diag(t):
        c, kb = TILES[t]
        return kb >= HB * c

    ctx = ExitStack()
    with ctx:
        def sb(name, shape, dt=F32):
            return ctx.enter_context(nc.sbuf_tensor(name, shape, dt))

        def sem(name):
            return ctx.enter_context(nc.semaphore(name))

        x_sb = sb("x_sb", [P, NB, D])
        xn_sb = sb("xn_sb", [P, NB, D])
        xnT = sb("xnT", [P, NB * P])
        xT_cur = [sb(f"xT_cur{p}", [P, S]) for p in range(2)]
        wq_cur = [sb(f"wq_cur{p}", [P, P]) for p in range(2)]
        wk_cur = [sb(f"wk_cur{p}", [P, P]) for p in range(2)]
        wv_cur = [sb(f"wv_cur{p}", [P, P]) for p in range(2)]
        wo_cur = sb("wo_cur", [P, P])
        q12 = [[sb(f"q12_{p}{h}", [P, S], F32R) for h in range(2)] for p in range(2)]
        q1m = [[sb(f"q1m_{p}{h}", [DH + 1, S], F32R) for h in range(2)] for p in range(2)]
        k11 = [[sb(f"k11_{p}{h}", [P, S], F32R) for h in range(2)] for p in range(2)]
        k2n = [[sb(f"k2n_{p}{h}", [DH + 1, S], F32R) for h in range(2)] for p in range(2)]
        v_sb = [sb(f"v_{p}", [P, KB, 2, DH]) for p in range(2)]
        NPROB = 4
        prob = [sb(f"prob_{n}", [P, 2, HALF]) for n in range(NPROB)]
        pv_raw = [sb(f"pv_raw_{c}", [P, HALF]) for c in range(2)]
        psumd = [sb(f"psumd_{c}", [P, 2, HALF]) for c in range(2)]
        lnden = sb("lnden", [P, HALF])
        rden = [sb(f"rden{n}", [P, HALF]) for n in range(3)]
        o_sb = [sb(f"o_{c}", [P, HALF]) for c in range(2)]
        rowmax = [sb(f"rowmax_{p}", [P, 2, KB]) for p in range(2)]
        rowmax2 = [sb(f"rowmax2_{p}", [P, 2, HB]) for p in range(2)]
        maxrow = sb("maxrow", [2 * KB, P], F32R)
        tab_cur = [sb(f"tab_{p}", [P, 2, KB, 2]) for p in range(2)]
        ident = sb("ident", [P, P])
        ident_b = sb("ident_b", [P, P], BF16)
        causal_b = sb("causal_b", [P, P], BF16)
        causal_t = sb("causal_t", [P, P], BF16)
        ones = sb("ones", [P, DH])
        key_no = sb("key_no", [P, KB])
        span_b = sb("span_b", [P, H])
        mask = sb("mask", [P, NPB, KB, 2])
        wrec = sb("wrec", [P, NPB, KB, 2])
        wgt = sb("wgt", [P, NPB, KB, 2])
        table = sb("table", [P, NPB, 2, KB, 2])
        tern_i = sb("tern_i", [P, P], I32)
        tern = sb("tern", [P, P])
        ternT = sb("ternT", [P, P])
        bias_b = sb("bias_b", [P, P])
        scale_b = sb("scale_b", [P, 1])
        sc = sb("sc", [P, 8])
        fq = sb("fq", [P, P])
        over = sb("over", [P, 2, P], U32)
        big = sb("big", [P, 2, P])
        stats = sb("stats", [P, NB, 6])
        mv = sb("mv", [P, NB, 2])
        vpe = sb("vpe", [P, NB])
        std = sb("std", [P, NB])
        rstd = sb("rstd", [P, NB])
        tmp = sb("tmp", [P, NB])

        NSCORE = 3
        scores = ctx.enter_context(nc.psum_tensor("scores", [P, NSCORE, HALF], F32))
        rings = {r: ctx.enter_context(nc.psum_tensor(f"ring_{r}", [P, 2, HALF], F32)) for r in "AM"}
        pv = ctx.enter_context(nc.psum_tensor("pv", [P, HALF], F32))

        x_landed = [sem(f"x_landed{b}") for b in range(B)]
        small_landed = sem("small_landed")
        wqkv_landed = [sem(f"wqkv_landed{p}") for p in range(2)]
        xT_landed = [sem(f"xT_landed{p}") for p in range(2)]
        wo_landed = sem("wo_landed")
        maxrow_landed = sem("maxrow_landed")
        out_stored = sem("out_stored")
        consts_done = sem("consts_done")
        pool_step = sem("pool_step")
        bias_added = sem("bias_added")
        tab_done = sem("tab_done")
        acc_done = sem("acc_done")
        var_done = sem("var_done")
        std_done = sem("std_done")
        wgt_done = sem("wgt_done")
        ln_done = sem("ln_done")
        xn_done = sem("xn_done")
        dve_step = sem("dve_step")
        table_done = sem("table_done")
        tern_done = sem("tern_done")
        fq_step = sem("fq_step")
        scores_ready = sem("scores_ready")
        exp_done = sem("exp_done")
        pv_done = sem("pv_done")
        norm_done = sem("norm_done")
        hi_done = sem("hi_done")
        raw_done = sem("raw_done")
        ready = {r: sem(f"ready_{r}") for r in "AM"}
        free = {r: sem(f"free_{r}") for r in "AM"}
        max_done = sem("max_done")
        lnden_done = sem("lnden_done")
        recip_done = sem("recip_done")
        newton_done = sem("newton_done")
        apart = sem("apart")

        block = ctx.enter_context(nc.Block())

        NCONST = 12
        FQ_STEPS = 7
        XT_READY = 2

        def wait_apart(engine, sem, value):
            engine.wait_ge(sem, value)
            engine.sem_inc(apart, 1)

        def index(i, name):
            return ring_index(i, name, NP)

        def prep_index(i, name):
            if isinstance(i, int) and i == 0:
                return PROLOGUE[ring_of(name)].index(name)
            return index(i - 1, name)

        TAIL = index(NP - 1, LAST["A"][-1]) + 1
        TAIL_BANK = len(LAST["A"]) % 2

        @block.sync
        def _(sp):
            for b in range(B):
                sp.dma_start(x_sb[:, b * KB:(b + 1) * KB, :],
                             x_dram[b, :, :].rearrange("(n p) d -> p n d", p=P)).then_inc(x_landed[b], 16)

            def load_qkv(i, p):
                hp = i % NPB
                b = i // NPB
                for w, dst in ((wq_dram, wq_cur), (wk_dram, wk_cur), (wv_dram, wv_cur)):
                    sp.dma_start(dst[p][:, :], w[:, bass.ds(hp * P, P)]).then_inc(wqkv_landed[p], 16)
                sp.dma_start(xT_cur[p][:, :], xnT[:, bass.ds(b * S, S)]).then_inc(xT_landed[p], 16)

            def load_wo(i):
                sp.dma_start(wo_cur[:, :], wo_dram[bass.ds((i % NPB) * P, P), :]).then_inc(wo_landed, 16)

            def place_maxrow(i, p):
                sp.wait_ge(free["A"], prep_index(i, "T") + 1)
                for h in range(2):
                    sp.dma_start(q1m[p][h][DH:DH + 1, :].bitcast(F32),
                                 maxrow[h * KB:(h + 1) * KB, :].bitcast(F32)).then_inc(maxrow_landed, 16)

            sp.wait_ge(free["A"], XT_READY)
            load_qkv(0, 0)
            load_wo(0)
            load_qkv(1, 1)
            place_maxrow(0, 0)
            sp.wait_ge(free["A"], len(TURNS))
            sp.wait_ge(ready["A"], prep_index(0, "V1") + 1)
            load_qkv(2, 0)
            place_maxrow(1, 1)

            def pair(i, p, last=False, load=True):
                if load:
                    sp.wait_ge(ready["A"], index(i - 1, "V1") + 1)
                    load_qkv(i + 2, p)
                sp.wait_ge(ready["A"], index(i, "Y1p") + 1)
                load_wo(i)
                if not last:
                    place_maxrow(i + 1, 1 - p)

            with sp.Fori(0, (NP - 2) // 2 - 1) as j:
                pair(2 * j + 1, 1)
                pair(2 * j + 2, 0)
            pair(NP - 3, 1)
            pair(NP - 2, 0, load=False)
            pair(NP - 1, 1, last=True, load=False)
            sp.wait_ge(free["A"], TAIL + 2)
            for b in range(B):
                sp.dma_start(out_dram[b, :, :].rearrange("(n p) d -> p n d", p=P),
                             x_sb[:, b * KB:(b + 1) * KB, :]).then_inc(out_stored, 16)
            sp.wait_ge(out_stored, 16 * B)

        @block.gpsimd
        def _(pool):
            g = nc.gpsimd
            g.memset(ident[:, :], 0.0).then_inc(pool_step, 1)
            g.memset(ident_b[:, :], 0.0).then_inc(pool_step, 1)
            g.memset(causal_b[:, :], 0.0).then_inc(pool_step, 1)
            g.memset(causal_t[:, :], 0.0).then_inc(pool_step, 1)
            g.memset(ones[:, :], 1.0).then_inc(consts_done, 1)
            g.memset(big[:, 0, :], 1e4).then_inc(consts_done, 1)
            g.memset(big[:, 1, :], -1e4).then_inc(consts_done, 1)
            g.iota(key_no[:, :], [[P, KB]], base=0, channel_multiplier=1,
                   allow_small_or_imprecise_dtypes=True).then_inc(consts_done, 1)
            pool.wait_ge(pool_step, 4)
            g.affine_select(out=ident[:, :], in_=ident[:, :], compare_op=ALU.not_equal, fill=1.0,
                            base=0, pattern=[[-1, P]], channel_multiplier=1).then_inc(consts_done, 1)
            g.affine_select(out=ident_b[:, :], in_=ident_b[:, :], compare_op=ALU.not_equal, fill=1.0,
                            base=0, pattern=[[-1, P]], channel_multiplier=1).then_inc(consts_done, 1)
            g.affine_select(out=causal_b[:, :], in_=causal_b[:, :], compare_op=ALU.is_ge, fill=MASKED,
                            base=0, pattern=[[-1, P]], channel_multiplier=1).then_inc(consts_done, 1)
            g.affine_select(out=causal_t[:, :], in_=causal_t[:, :], compare_op=ALU.is_ge, fill=MASKED,
                            base=0, pattern=[[1, P]], channel_multiplier=-1).then_inc(consts_done, 1)
            pool.wait_ge(xn_done, NB)
            pool.wait_ge(small_landed, 64)
            g.tensor_tensor(x_sb[:, :, :], x_sb[:, :, :], bias_b[:, :].unsqueeze(1).to_broadcast([P, NB, P]),
                            ALU.add).then_inc(bias_added, 1)

            def pair_table(i, p):
                g.tensor_copy(tab_cur[p][:, :, :, :],
                              table[:, bass.ds(i % NPB, 1), :, :, :].rearrange("p o a k h -> p (o a) k h")
                              ).then_inc(tab_done, 1)

            pool.wait_ge(table_done, 1)
            pair_table(0, 0)

            def pair(i, p, last=False):
                if not last:
                    pair_table(i + 1, 1 - p)
                for t in range(NT):
                    c, kb = TILES[t]
                    lo = first_col(t)
                    pr = prob[t % NPROB]
                    if kb == 0 and not (isinstance(i, int) and i == 0):
                        pool.wait_ge(ready["A"], (index(i - 1, "D0") if c == 0 else index(i, "D1p")) + 1)
                    if t == 0:
                        wait_apart(pool, exp_done, (i * NT + (t + 1)) * 2)
                    else:
                        pool.wait_ge(exp_done, (i * NT + (t + 1)) * 2)
                    acc = psumd[c]
                    if kb == 0:
                        if c == 0:
                            g.tensor_scalar(acc[:, :, 0:P], pr[:, :, 0:P], 1.0, None, ALU.mult)
                    elif kb == 1:
                        g.tensor_tensor(acc[:, :, lo:HALF], prob[(t - 1) % NPROB][:, :, lo:HALF],
                                        pr[:, :, lo:HALF], ALU.add).then_inc(acc_done, 2)
                    else:
                        pool.wait_ge(acc_done, i * NT + t)
                        g.tensor_tensor(acc[:, :, lo:HALF], acc[:, :, lo:HALF], pr[:, :, lo:HALF],
                                        ALU.add).then_inc(acc_done, 1)

            pair(0, 0)
            with pool.Fori(0, (NP - 2) // 2) as j:
                pair(2 * j + 1, 1)
                pair(2 * j + 2, 0)
            pair(NP - 1, 1, last=True)

        @block.scalar
        def _(act):
            a = nc.scalar
            for dst, src in ((span_b[:, :], span_dram.rearrange("a h b c -> (a b c) h").to_broadcast([P, H])),
                             (bias_b[:, :], bias_dram.unsqueeze(0).to_broadcast([P, P])),
                             (scale_b[:, :], scale_dram.to_broadcast([P, 1])),
                             (tern_i[:, :], tern_dram[:, :])):
                act.dma_start(dst, src).then_inc(small_landed, 16)
            act.wait_ge(var_done, 1)
            a.activation(std[:, :], vpe[:, :], ACT.Sqrt).then_inc(std_done, 1)
            nc.scalar.preload_act_table_set("natural_log_exp_and_others")
            act.wait_ge(wgt_done, 1)
            a.activation(table[:, :, 0, :, :], wgt[:, :, :, :], ACT.Ln).then_inc(ln_done, 1)

            def exps(i, p, t):
                lo = first_col(t)
                if not (isinstance(i, int) and i == 0 and t < NPROB):
                    act.wait_ge(pv_done, i * NT + (t - NPROB + 1))
                    act.wait_ge(acc_done, i * NT + (t - NPROB + 1))
                if t == 0:
                    act.wait_ge(tab_done, i + 1)
                kb = TILES[t][1]
                for h in range(2):
                    act.wait_ge(scores_ready, i * (2 * NT) + (2 * t + h + 1))
                    a.activation(prob[t % NPROB][:, h, lo:HALF], scores[:, (2 * t + h) % NSCORE, lo:HALF],
                                 ACT.Exp, bias=tab_cur[p][:, 0, kb, h:h + 1], scale=1.0 / DH
                                 ).then_inc(exp_done, 1)

            def pv_out(i, c):
                act.wait_ge(pv_done, i * NT + (HB if c == 0 else NT))
                if not (isinstance(i, int) and i == 0):
                    act.wait_ge(norm_done, i * 2 + (c - 1))
                a.activation(pv_raw[c][:, :], pv[:, :], ACT.Copy).then_inc(raw_done, 1)

            def reciprocal(i, c, n, r):
                act.wait_ge(ready["A"], n + 1)
                a.activation(lnden[:, :], rings["A"][:, r, :], ACT.Ln).then_inc(lnden_done, 1)
                act.wait_ge(lnden_done, i * 2 + (c + 1))
                a.activation(rden[0][:, :], lnden[:, :], ACT.Exp, scale=-1.0).then_inc(recip_done, 1)

            def high_parts(i, p, name, r):
                act.wait_ge(ready["A"], prep_index(i, name) + 1)
                cols = slice(int(name[1]) * HALF, (int(name[1]) + 1) * HALF)
                for h in range(2):
                    src = rings["A"][h * DH:(h + 1) * DH, r, :]
                    if name[0] == "Q":
                        a.activation(q1m[p][h][0:DH, cols], src, ACT.Copy)
                        a.activation(q12[p][h][0:DH, cols], src, ACT.Copy).then_inc(hi_done, 1)
                    else:
                        a.activation(k11[p][h][0:DH, cols], src, ACT.Copy)
                        a.activation(k11[p][h][DH:P, cols], src, ACT.Copy).then_inc(hi_done, 1)

            for u in of_prep(DVE_PLAN):
                if u[0] in "QK":
                    high_parts(0, 0, u, bank(u, PROLOGUE))

            def pair(i, p, where=STEADY):
                for u in kept(ACT_PLAN, where is FIRST, where is LAST):
                    if u[0] == "e":
                        exps(i, p, int(u[1:]))
                    elif u == "P1p":
                        pv_out(i - 1, 1)
                    elif u == "P0":
                        pv_out(i, 0)
                    elif u == "D0":
                        reciprocal(i, 0, index(i, u), bank(u, where))
                    elif u == "D1p":
                        reciprocal(i - 1, 1, index(i, u), bank(u, where))
                    else:
                        high_parts(i + 1, 1 - p, u, bank(u, where))

            pair(0, 0, FIRST)
            with act.Fori(0, (NP - 2) // 2) as j:
                pair(2 * j + 1, 1)
                pair(2 * j + 2, 0)
            pair(NP - 1, 1, LAST)
            pv_out(NP - 1, 1)
            reciprocal(NP - 1, 1, TAIL, TAIL_BANK)

        @block.vector
        def _(dve):
            v = nc.vector
            steps = [0]

            def then(ins):
                steps[0] += 1
                ins.then_inc(dve_step, 1)
                dve.wait_ge(dve_step, steps[0])

            for p in range(2):
                for h in range(2):
                    v.memset(k2n[p][h][DH:DH + 1, :].bitcast(F32), -1.0).then_inc(consts_done, 1)
            for b in range(B):
                dve.wait_ge(x_landed[b], 16)
                for n in range(b * KB, (b + 1) * KB):
                    last = v.bn_stats(stats[:, n, :], x_sb[:, n, :])
            then(last)
            for n in range(NB):
                last = v.bn_aggr(mv[:, n, :], stats[:, n, :])
            then(last)
            v.tensor_scalar(vpe[:, :], mv[:, :, 1], EPS_LN, None, ALU.add).then_inc(var_done, 1)
            dve.wait_ge(consts_done, NCONST)
            dve.wait_ge(small_landed, 64)
            then(v.tensor_scalar(span_b[:, :], span_b[:, :], float(S), None, ALU.mult))
            for h in range(H):
                last = v.tensor_scalar(mask[:, h // 2, :, h % 2], key_no[:, :], span_b[:, h:h + 1],
                                       1.0 / (RAMP + 1), ALU.add, ALU.mult)
            then(last)
            then(v.tensor_scalar(mask[:, :, :, :], mask[:, :, :, :], 0.0, 1.0, ALU.max, ALU.min))
            v.tensor_scalar(wgt[:, :, :, :], mask[:, :, :, :], EPS_SUM, None, ALU.add).then_inc(wgt_done, 1)
            dve.wait_ge(std_done, 1)
            then(v.reciprocal(rstd[:, :], std[:, :]))
            then(v.tensor_tensor(tmp[:, :], rstd[:, :], rstd[:, :], ALU.mult))
            then(v.tensor_tensor(tmp[:, :], tmp[:, :], vpe[:, :], ALU.mult))
            then(v.tensor_scalar(tmp[:, :], tmp[:, :], -0.5, 1.5, ALU.mult, ALU.add))
            then(v.tensor_tensor(rstd[:, :], rstd[:, :], tmp[:, :], ALU.mult))

            def normalise(b):
                for n in range(b * KB, (b + 1) * KB):
                    v.tensor_scalar(xn_sb[:, n, :], x_sb[:, n, :], mv[:, n, 0:1], rstd[:, n:n + 1],
                                    ALU.subtract, ALU.mult).then_inc(xn_done, 1)

            def turned(n):
                dve.wait_ge(ready["A"], n + 1)
                v.tensor_copy(xnT[:, n * HALF:(n + 1) * HALF], rings["A"][:, n % 2, :]).then_inc(free["A"], 1)

            for b in range(B):
                normalise(b)
                if b == 0:
                    dve.wait_ge(wgt_done, 1)
                    then(v.reciprocal(wrec[:, :, :, :], wgt[:, :, :, :]))
                    dve.wait_ge(ln_done, 1)
                    v.tensor_tensor(table[:, :, 1, :, :], mask[:, :, :, :], wrec[:, :, :, :],
                                    ALU.mult).then_inc(table_done, 1)
                for n in (2 * b, 2 * b + 1):
                    turned(n)
            then(v.tensor_scalar(sc[:, 0:1], scale_b[:, :], 1e-5, None, ALU.max))
            v.memset(sc[:, 2:3], 0.0)
            v.memset(sc[:, 3:4], 1.0)
            then(v.tensor_scalar(sc[:, 4:5].bitcast(U32), scale_b[:, :], FLT_MAX, None, ALU.is_le))
            v.copy_predicated(sc[:, 2:3], sc[:, 4:5].bitcast(U32), sc[:, 0:1])
            then(v.copy_predicated(sc[:, 3:4], sc[:, 4:5].bitcast(U32), sc[:, 0:1]))
            then(v.reciprocal(sc[:, 5:6], sc[:, 3:4]))
            v.tensor_scalar(tern[:, :], tern_i[:, :], -1.0, None, ALU.add).then_inc(tern_done, 1)

            def low_parts(i, p, name, r):
                before = i * 8 + 2 * [u for u in of_prep(DVE_PLAN) if u[0] in "QK"].index(name)
                cols = slice(int(name[1]) * HALF, (int(name[1]) + 1) * HALF)
                for h in range(2):
                    src = rings["A"][h * DH:(h + 1) * DH, r, :]
                    dve.wait_ge(hi_done, before + (h + 1))
                    if name[0] == "Q":
                        last = v.tensor_tensor(q12[p][h][DH:P, cols], src,
                                               q1m[p][h][0:DH, cols].bitcast(F32), ALU.subtract)
                    else:
                        last = v.tensor_tensor(k2n[p][h][0:DH, cols], src,
                                               k11[p][h][0:DH, cols].bitcast(F32), ALU.subtract)
                last.then_inc(free["A"], 1)

            def prep_unit(i, p, name, r):
                if name[0] in "QK":
                    low_parts(i, p, name, r)
                    return
                dve.wait_ge(ready[ring_of(name)], prep_index(i, name) + 1)
                if name[0] == "M":
                    j, k0, n, heads = MAX_UNITS[int(name[1:])]
                    dst = rowmax[p][:, :, j] if k0 == 0 else rowmax2[p][:, :, j - HB]
                    v.tensor_reduce(dst[:, heads[0]:heads[-1] + 1],
                                    rings["M"][:, r, 0:n * len(heads)].rearrange("p (h k) -> p h k", k=n),
                                    axis=AX, op=ALU.max).then_inc(free["M"], 1)
                    if name == M[-1]:
                        dve.wait_ge(free["M"], prep_index(i, name) + 1)
                        v.tensor_tensor(rowmax[p][:, :, HB:KB], rowmax[p][:, :, HB:KB],
                                        rowmax2[p][:, :, :], ALU.max).then_inc(max_done, 1)
                elif name == "T":
                    v.tensor_copy(maxrow[:, :], rings["A"][0:2 * KB, r, 0:P]).then_inc(free["A"], 1)
                else:
                    if name == "V0":
                        dve.wait_ge(tab_done, i + 1)
                    b0 = HB * int(name[1])
                    v.tensor_tensor(v_sb[p][:, b0:b0 + HB, :, :],
                                    rings["A"][:, r, :].rearrange("p (k h d) -> p k h d", k=HB, h=2),
                                    tab_cur[p][:, 1, b0:b0 + HB, :].unsqueeze(3).to_broadcast([P, HB, 2, DH]),
                                    ALU.mult).then_inc(free["A"], 1)

            for u in of_prep(DVE_PLAN):
                prep_unit(0, 0, u, bank(u, PROLOGUE))
            dve.wait_ge(ready["A"], len(PROLOGUE["A"]))
            v.tensor_copy(ternT[:, :], rings["A"][:, bank("W", PROLOGUE), 0:P]).then_inc(free["A"], 1)
            dve.wait_ge(bias_added, 1)

            def quantise(i, step):
                if step > FQ_STEPS - 2:
                    wait_apart(dve, fq_step, i * FQ_STEPS + (step - 1))
                elif step > 1:
                    dve.wait_ge(fq_step, i * FQ_STEPS + (step - 1))
                if step == 1:
                    ins = v.tensor_scalar(fq[:, :], xnT[:, bass.ds(i * P, P)], sc[:, 5:6], ACT_QB,
                                          ALU.mult, ALU.min)
                elif step == 2:
                    ins = v.tensor_scalar(fq[:, :], fq[:, :], -ACT_QB, ROUND, ALU.max, ALU.add)
                elif step == 3:
                    ins = v.tensor_scalar(fq[:, :], fq[:, :], -ROUND, sc[:, 2:3], ALU.add, ALU.mult)
                elif step == 4:
                    ins = v.tensor_scalar(over[:, 0, :], fq[:, :], FLT_MAX, None, ALU.is_gt)
                elif step == 5:
                    ins = v.tensor_scalar(over[:, 1, :], fq[:, :], -FLT_MAX, None, ALU.is_lt)
                elif step == 6:
                    ins = v.copy_predicated(fq[:, :], over[:, 0, :], big[:, 0, :])
                else:
                    ins = v.copy_predicated(fq[:, :], over[:, 1, :], big[:, 1, :])
                ins.then_inc(fq_step, 1)

            def normalise_pv(i, c, n, r):
                dve.wait_ge(recip_done, i * 2 + (c + 1))
                v.tensor_tensor(rden[1][:, :], rings["A"][:, r, :], rden[0][:, :], ALU.mult
                                ).then_inc(free["A"], 1)
                dve.wait_ge(free["A"], n + 1)
                v.scalar_tensor_tensor(out=rden[2][:, :], in0=rden[1][:, :], scalar=2.0, in1=rden[0][:, :],
                                       op0=ALU.subtract, op1=ALU.mult).then_inc(newton_done, 1)
                dve.wait_ge(newton_done, i * 2 + (c + 1))
                dve.wait_ge(raw_done, i * 2 + (c + 1))
                v.scalar_tensor_tensor(out=o_sb[c][:, :], in0=pv_raw[c][:, :], scalar=-1.0,
                                       in1=rden[2][:, :], op0=ALU.mult, op1=ALU.mult).then_inc(norm_done, 1)

            def add_output(i, c, n, r):
                dve.wait_ge(ready["A"], n + 1)
                rows = x_sb[:, bass.ds((i // NPB) * KB + c * HB, HB), :]
                v.tensor_tensor(rows, rows, rings["A"][:, r, :].rearrange("p (n d) -> p n d", n=HB),
                                ALU.add).then_inc(free["A"], 1)

            def pair(i, p, where=STEADY):
                for u in kept(DVE_PLAN, where is FIRST, where is LAST):
                    if u[0] == "q":
                        quantise(i, int(u[1:]))
                        continue
                    r = bank(u, where)
                    if u == "D0":
                        normalise_pv(i, 0, index(i, u), r)
                    elif u == "D1p":
                        normalise_pv(i - 1, 1, index(i, u), r)
                    elif u == "Y0":
                        add_output(i, 0, index(i, u), r)
                    elif u == "Y1p":
                        add_output(i - 1, 1, index(i, u), r)
                    elif u == "F":
                        dve.wait_ge(ready["A"], index(i, u) + 1)
                        rows = x_sb[:, bass.ds(i, 1), :]
                        v.tensor_tensor(rows, rows, rings["A"][:, r, 0:P].unsqueeze(1), ALU.add
                                        ).then_inc(free["A"], 1)
                    else:
                        prep_unit(i + 1, 1 - p, u, r)

            pair(0, 0, FIRST)
            with dve.Fori(0, (NP - 2) // 2) as j:
                pair(2 * j + 1, 1)
                pair(2 * j + 2, 0)
            pair(NP - 1, 1, LAST)
            normalise_pv(NP - 1, 1, TAIL, TAIL_BANK)
            add_output(NP - 1, 1, TAIL + 1, 1 - TAIL_BANK)

        @block.tensor
        def _(pe):
            t_ = nc.tensor
            pe.wait_ge(consts_done, NCONST)

            def begin_unit(ring, n):
                if not isinstance(n, int) or n >= 2:
                    pe.wait_ge(free[ring], n - 1)

            for n in range(len(TURNS)):
                begin_unit("A", n)
                pe.wait_ge(xn_done, HB * (n + 1))
                for k in range(HB):
                    last = t_.transpose(rings["A"][:, n % 2, k * P:(k + 1) * P], xn_sb[:, n * HB + k, :],
                                        ident[:, :])
                last.then_inc(ready["A"], 1)

            def prep_unit(i, p, name, r):
                ring = rings[ring_of(name)]
                begin_unit(ring_of(name), prep_index(i, name))
                if name == "Q0":
                    pe.wait_ge(wqkv_landed[p], (i - p) * 24 + 48)
                    pe.wait_ge(xT_landed[p], (i - p) * 8 + 16)
                if name[0] in "QK":
                    c = int(name[1])
                    w = wq_cur if name[0] == "Q" else wk_cur
                    last = t_.matmul(ring[:, r, :], w[p][:, :], xT_cur[p][:, c * HALF:(c + 1) * HALF],
                                     start=True, stop=True)
                elif name[0] == "V":
                    for k in range(HB):
                        kb = HB * int(name[1]) + k
                        last = t_.matmul(ring[:, r, k * P:(k + 1) * P], xT_cur[p][:, kb * P:(kb + 1) * P],
                                         wv_cur[p][:, :], start=True, stop=True)
                elif name[0] == "M":
                    need = {M[0]: "K0", M[6]: "Q1", M[14]: "K1"}.get(name)
                    if need:
                        pe.wait_ge(free["A"], prep_index(i, need) + 1)
                    j, k0, w, heads = MAX_UNITS[int(name[1:])]
                    for at, h in enumerate(heads):
                        out = ring[:, r, at * w:(at + 1) * w]
                        diag = k0 + w == (j + 1) * P
                        last = t_.matmul(out, q12[p][h][:, j * P:(j + 1) * P], k11[p][h][:, k0:k0 + w],
                                         start=True, stop=not diag)
                        if diag:
                            last = t_.matmul(ring[:, r, (at + 1) * w - P:(at + 1) * w], ident_b[:, :],
                                             causal_b[:, :], start=False, stop=True)
                else:
                    pe.wait_ge(max_done, i + 1)
                    last = t_.matmul(ring[0:2 * KB, r, 0:P], rowmax[p][:, :, :].rearrange("p h j -> p (h j)"),
                                     ident[:, :], start=True, stop=True)
                last.then_inc(ready[ring_of(name)], 1)

            for u in of_prep(PE_ORDER):
                prep_unit(0, 0, u, bank(u, PROLOGUE))
            begin_unit("A", PROLOGUE["A"].index("W"))
            pe.wait_ge(tern_done, 1)
            t_.transpose(rings["A"][:, bank("W", PROLOGUE), 0:P], tern[:, :], ident[:, :]
                         ).then_inc(ready["A"], 1)

            def denominators(i, c, r):
                pe.wait_ge(acc_done, i * NT + (HB if c == 0 else NT))
                for h in range(2):
                    last = t_.matmul(rings["A"][h * DH:(h + 1) * DH, r, :], ones[:, :], psumd[c][:, h, :],
                                     start=True, stop=True)
                last.then_inc(ready["A"], 1)

            def output_projection(i, c, r):
                pe.wait_ge(norm_done, i * 2 + (c + 1))
                pe.wait_ge(wo_landed, (i + 1) * 16)
                for k in range(HB):
                    last = t_.matmul(rings["A"][:, r, k * P:(k + 1) * P], o_sb[c][:, k * P:(k + 1) * P],
                                     wo_cur[:, :], start=True, stop=True)
                last.then_inc(ready["A"], 1)

            def own_unit(i, name, r):
                begin_unit("A", index(i, name))
                if name == "D0":
                    denominators(i, 0, r)
                elif name == "D1p":
                    denominators(i - 1, 1, r)
                elif name == "Y0":
                    output_projection(i, 0, r)
                elif name == "Y1p":
                    output_projection(i - 1, 1, r)
                else:
                    pe.wait_ge(fq_step, (i + 1) * FQ_STEPS)
                    t_.matmul(rings["A"][:, r, 0:P], fq[:, :], ternT[:, :], start=True, stop=True
                              ).then_inc(ready["A"], 1)

            def scores_of(i, p, t, h):
                c, kb = TILES[t]
                lo = first_col(t)
                cols = slice(c * HALF + lo, (c + 1) * HALF)
                n = 2 * t + h
                if not (isinstance(i, int) and i == 0 and n < NSCORE):
                    pe.wait_ge(exp_done, i * (2 * NT) + (n - NSCORE + 1))
                if t == 0 and h == 0:
                    pe.wait_ge(maxrow_landed, (i + 1) * 32)
                out = scores[:, n % NSCORE, lo:HALF]
                keys = slice(kb * P, (kb + 1) * P)
                t_.matmul(out, k11[p][h][:, keys], q12[p][h][:, cols], start=True, stop=False)
                if is_diag(t):
                    t_.matmul(scores[:, n % NSCORE, lo:lo + P], ident_b[:, :], causal_t[:, :],
                              start=False, stop=False)
                t_.matmul(out, k2n[p][h][:, keys], q1m[p][h][:, cols], start=False, stop=True
                          ).then_inc(scores_ready, 1)

            def pv_of(i, p, t):
                c, kb = TILES[t]
                lo = first_col(t)
                pe.wait_ge(exp_done, i * (2 * NT) + 2 * (t + 1))
                if kb == 0 and not (isinstance(i, int) and i == 0 and c == 0):
                    pe.wait_ge(raw_done, i * 2 + c)
                if t == 0:
                    pe.wait_ge(free["A"], prep_index(i, "V1") + 1)
                for h in range(2):
                    last = t_.matmul(pv[h * DH:(h + 1) * DH, lo:HALF], v_sb[p][:, kb, h, :],
                                     prob[t % NPROB][:, h, lo:HALF], start=(kb == 0),
                                     stop=(kb == HB * (c + 1) - 1))
                last.then_inc(pv_done, 1)

            def pair(i, p, where=STEADY):
                for u in kept(PE_LEAD, where is FIRST, where is LAST):
                    prep_unit(i + 1, 1 - p, u, bank(u, where))
                scores_of(i, p, 0, 0)
                scores_of(i, p, 0, 1)
                for s in range(NT):
                    for place in range(3):
                        if place == 2:
                            pv_of(i, p, s)
                        elif s + 1 < NT:
                            scores_of(i, p, s + 1, place)
                        for u in kept(PE_PLAN[s][place], where is FIRST, where is LAST):
                            if u in OF_THIS_PAIR or u in OF_PAIR_BEFORE:
                                own_unit(i, u, bank(u, where))
                            else:
                                prep_unit(i + 1, 1 - p, u, bank(u, where))

            pair(0, 0, FIRST)
            with pe.Fori(0, (NP - 2) // 2) as j:
                pair(2 * j + 1, 1)
                pair(2 * j + 2, 0)
            pair(NP - 1, 1, LAST)
            begin_unit("A", TAIL)
            denominators(NP - 1, 1, TAIL_BANK)
            begin_unit("A", TAIL + 1)
            output_projection(NP - 1, 1, 1 - TAIL_BANK)


_INS = ["L0_attn_query", "L0_attn_Wq", "L0_attn_Wk", "L0_attn_Wv", "L0_attn_Wo", "L0_attn_span_val",
        "L0_ffn_ternary_weight", "L0_ffn_bias", "L0_ffn_act_scale"]


def kernel(**inputs):
    import concourse.bacc as bacc
    import numpy as np
    from concourse.bass_utils import run_bass_kernel_spmd

    nc = bacc.Bacc("TRN2", target_bir_lowering=False, num_devices=1)
    arrays, args = {}, []
    for name in _INS:
        a = np.ascontiguousarray(inputs[name])
        if a.ndim == 0:
            a = a.reshape(1, 1)
        arrays[f"in_{name}"] = a
        args.append(nc.dram_tensor(f"in_{name}", a.shape, mybir.dt.from_np(a.dtype), kind="ExternalInput").ap())
    shape = inputs["L0_attn_query"].shape
    args.append(nc.dram_tensor("out_0", shape, F32, kind="ExternalOutput").ap())
    attention_ffn(nc, *args)
    r = run_bass_kernel_spmd(nc, [arrays], core_ids=[0])
    return r.results[0]["out_0"]
```

```python
from contextlib import ExitStack

import concourse.bass as bass
from concourse import mybir

ALU = mybir.AluOpType
ACT = mybir.ActivationFunctionType
AX = mybir.AxisListType.X
F32 = mybir.dt.float32
F32R = mybir.dt.float32r
BF16 = mybir.dt.bfloat16
I32 = mybir.dt.int32
U32 = mybir.dt.uint32

P = 128
HALF = 512
RAMP = 32
EPS_LN = 1e-5
EPS_SUM = 1e-8
ACT_QB = 127.0
ROUND = 12582912.0
FLT_MAX = 3.4028234663852886e38
MASKED = -1e30

MAX_UNITS = (
    [(0, 0, 128, (0, 1)), (1, 0, 256, (0, 1))]
    + [(j, 0, 128 * (j + 1), (h,)) for j in (2, 3) for h in (0, 1)]
    + [(j, 0, 512, (h,)) for j in (4, 5, 6, 7) for h in (0, 1)]
    + [(4, 512, 128, (0, 1)), (5, 512, 256, (0, 1))]
    + [(j, 512, 128 * (j - 3), (h,)) for j in (6, 7) for h in (0, 1)]
)
M = [f"M{n}" for n in range(len(MAX_UNITS))]

PE_LEAD = ["Q0", "K0"]
PE_PLAN = [
    [["D1p"], [], []],
    [[], ["M0", "M1"], []],
    [["M2"], ["Q1", "M3"], []],
    [[], ["Y1p"], ["M4"]],
    [["K1"], ["M5"], ["M6"]],
    [["M7"], ["V0"], ["D0", "M8", "M9"]],
    [[], [], ["M10", "M11"]],
    [[], [], ["V1"]],
    [["M12"], ["M13"], ["M14", "M15"]],
    [["M16", "F"], ["M17", "M18"], ["M19"]],
    [[], [], ["T"]],
    [[], ["Y0"], []],
]
DVE_PLAN = [
    "Q0", "q1", "q2", "K0", "q3", "M0", "M1", "q4", "D1p", "M2", "M3", "Q1", "q5", "Y1p", "M4", "M5",
    "M6", "K1", "q6", "q7", "M7", "M8", "M9", "V0", "M10", "M11", "D0", "M12", "M13", "V1", "M14",
    "M15", "M16", "M17", "M18", "F", "M19", "T", "Y0",
]
ACT_PLAN = [
    "P1p", "Q0", "e0", "K0", "e1", "D1p", "e2", "e3", "Q1", "e4", "P0", "e5", "K1", "e6", "D0", "e7",
    "e8", "e9", "e10", "e11",
]
OF_PAIR_BEFORE = ("D1p", "Y1p", "P1p")
OF_THIS_PAIR = ("D0", "Y0", "F", "P0") + tuple(f"q{n}" for n in range(1, 8)) + tuple(f"e{n}" for n in range(12))


def kept(units, first, last):
    return [u for u in units if not (first and u in OF_PAIR_BEFORE)
            and not (last and u not in OF_THIS_PAIR + OF_PAIR_BEFORE)]


def of_prep(units):
    return [u for u in units if u not in OF_THIS_PAIR + OF_PAIR_BEFORE]


def ring_of(name):
    return "M" if name[0] == "M" else "A"


def in_ring(ring, units):
    return [u for u in units if ring_of(u) == ring]


PE_ORDER = PE_LEAD + [u for slot in PE_PLAN for place in slot for u in place]
PREP0 = of_prep(PE_ORDER)
PREP0_DVE = of_prep(DVE_PLAN)


def insert_after(units, places):
    return [u for unit in units for u in [unit] + places.get(unit, [])]


PE_PROLOGUE = ["X0", "X1"] + insert_after(PREP0, {M[9]: ["X2", "X3"], M[15]: ["X4", "X5"],
                                                  M[19]: ["X6", "X7"]}) + ["W"]
DVE_PROLOGUE = insert_after(PREP0_DVE, {"K0": ["S1"], M[1]: ["S2"], M[3]: ["S3"], "Q1": ["R"], M[7]: ["N1"],
                                        M[13]: ["N2"], M[17]: ["N3"]})
PROLOGUE = {r: in_ring(r, [u for u in PE_PROLOGUE if u[0] != "X"]) for r in "AM"}
STEADY = {r: in_ring(r, PE_ORDER) for r in "AM"}
FIRST = {r: in_ring(r, kept(PE_ORDER, True, False)) for r in "AM"}
LAST = {r: in_ring(r, kept(PE_ORDER, False, True)) for r in "AM"}
assert all(len(units[r]) % 2 == 0 for units in (PROLOGUE, STEADY, FIRST) for r in "AM")


def ring_index(i, name, n_pairs):
    r = ring_of(name)
    if isinstance(i, int) and i == 0:
        return len(PROLOGUE[r]) + FIRST[r].index(name)
    before = len(PROLOGUE[r]) + len(FIRST[r]) - len(STEADY[r])
    if isinstance(i, int) and i == n_pairs - 1:
        return before + len(STEADY[r]) * i + LAST[r].index(name)
    return i * len(STEADY[r]) + (before + STEADY[r].index(name))


def bank(name, where):
    return where[ring_of(name)].index(name) % 2


def attention_ffn(nc, x_dram, wq_dram, wk_dram, wv_dram, wo_dram, span_dram, tern_dram, bias_dram,
                  scale_dram, out_dram):
    B, S, D = x_dram.shape
    H = span_dram.shape[1]
    DH = wq_dram.shape[1] // H
    NPB = H // 2
    NP = B * NPB
    KB = S // P
    HB = HALF // P
    NB = B * KB
    TILES = [(0, kb) for kb in range(HB)] + [(1, kb) for kb in range(KB)]
    NT = len(TILES)
    assert D == P and DH == 64 and S == 2 * HALF and NT == 12 and KB == 8 and NB == NP

    def first_col(t):
        c, kb = TILES[t]
        return max(0, kb - HB * c) * P

    def is_diag(t):
        c, kb = TILES[t]
        return kb >= HB * c

    diag_upto = [sum(is_diag(u) for u in range(t + 1)) for t in range(NT)]
    NDIAG = diag_upto[-1]

    ctx = ExitStack()
    with ctx:
        def sb(name, shape, dt=F32):
            return ctx.enter_context(nc.sbuf_tensor(name, shape, dt))

        def sem(name):
            return ctx.enter_context(nc.semaphore(name))

        x_sb = sb("x_sb", [P, NB, D])
        xn_sb = sb("xn_sb", [P, NB * P])
        x1T = sb("x1T", [P, NB * P], F32R)
        x2T = xn_sb
        x1_cur = sb("x1_cur", [P, S], F32R)
        x2_cur = sb("x2_cur", [P, S], F32R)
        xf_cur = sb("xf_cur", [P, S])
        w_in = [sb(f"w_in{p}", [P, 3, P]) for p in range(2)]
        w1 = [sb(f"w1_{p}", [P, 2, P], F32R) for p in range(2)]
        w2 = [sb(f"w2_{p}", [P, 2, P], F32R) for p in range(2)]
        wo_cur = sb("wo_cur", [P, P])
        q12 = [[sb(f"q12_{p}{h}", [P, S], F32R) for h in range(2)] for p in range(2)]
        q1m = [[sb(f"q1m_{p}{h}", [DH + 1, S], F32R) for h in range(2)] for p in range(2)]
        k11 = [[sb(f"k11_{p}{h}", [P, S], F32R) for h in range(2)] for p in range(2)]
        k2n = [[sb(f"k2n_{p}{h}", [DH + 1, S], F32R) for h in range(2)] for p in range(2)]
        v_sb = [sb(f"v_{p}", [P, KB, 2, DH]) for p in range(2)]
        NPROB = 4
        prob = [sb(f"prob_{n}", [P, 2, HALF]) for n in range(NPROB)]
        pv_raw = [sb(f"pv_raw_{c}", [P, HALF]) for c in range(2)]
        psumd = [sb(f"psumd_{c}", [P, 2, HALF]) for c in range(2)]
        lnden = sb("lnden", [P, HALF])
        rden = [sb(f"rden{n}", [P, HALF]) for n in range(3)]
        o_sb = [sb(f"o_{c}", [P, HALF]) for c in range(2)]
        rowmax = [sb(f"rowmax_{p}", [P, 2, KB]) for p in range(2)]
        rowmax2 = [sb(f"rowmax2_{p}", [P, 2, HB]) for p in range(2)]
        maxrow = sb("maxrow", [2 * KB, P], F32R)
        tab_cur = [sb(f"tab_{p}", [P, 2, KB, 2]) for p in range(2)]
        ident = sb("ident", [P, P])
        ident_b = sb("ident_b", [P, P], BF16)
        causal_b = sb("causal_b", [P, P], BF16)
        ones = sb("ones", [P, DH])
        key_no = sb("key_no", [P, KB])
        span_b = sb("span_b", [P, H])
        mask = sb("mask", [P, NPB, KB, 2])
        wrec = sb("wrec", [P, NPB, KB, 2])
        wgt = sb("wgt", [P, NPB, KB, 2])
        table = sb("table", [P, NPB, 2, KB, 2])
        tern_i = sb("tern_i", [P, P], I32)
        tern = sb("tern", [P, P])
        ternT = sb("ternT", [P, P])
        bias_b = sb("bias_b", [P, P])
        scale_b = sb("scale_b", [P, 1])
        sc = sb("sc", [P, 8])
        fx = sb("fx", [P, P])
        fq = sb("fq", [P, P])
        over = sb("over", [P, 2, P], U32)
        big = sb("big", [P, 2, P])
        stats = sb("stats", [P, NB, 6])
        mv = sb("mv", [P, NB, 2])
        vpe = sb("vpe", [P, NB])
        lnv = sb("lnv", [P, NB])
        rs0 = sb("rs0", [P, NB])
        rstd = sb("rstd", [P, NB])
        tmp = sb("tmp", [P, NB])

        NSCORE = 3
        scores = ctx.enter_context(nc.psum_tensor("scores", [P, NSCORE, HALF], F32))
        rings = {r: ctx.enter_context(nc.psum_tensor(f"ring_{r}", [P, 2, HALF], F32)) for r in "AM"}
        pv = ctx.enter_context(nc.psum_tensor("pv", [P, HALF], F32))

        x_landed = [sem(f"x_landed{b}") for b in range(B)]
        small_landed = sem("small_landed")
        wqkv_landed = [sem(f"wqkv_landed{p}") for p in range(2)]
        x_cur_landed = sem("x_cur_landed")
        w_split = sem("w_split")
        turned_ready = sem("turned_ready")
        turned_out = sem("turned_out")
        x1_done = sem("x1_done")
        x2_done = sem("x2_done")
        x2_rest_done = sem("x2_rest_done")
        rstd_done = sem("rstd_done")
        minus_ones_done = sem("minus_ones_done")
        span_landed = sem("span_landed")
        fx_done = sem("fx_done")
        wo_landed = sem("wo_landed")
        maxrow_landed = sem("maxrow_landed")
        out_stored = sem("out_stored")
        consts_done = sem("consts_done")
        pool_step = sem("pool_step")
        bias_added = sem("bias_added")
        tab_done = sem("tab_done")
        sel_done = sem("sel_done")
        acc_done = sem("acc_done")
        xf_done = sem("xf_done")
        var_done = sem("var_done")
        lnv_done = sem("lnv_done")
        rs0_done = sem("rs0_done")
        wgt_done = sem("wgt_done")
        ln_done = sem("ln_done")
        xn_done = sem("xn_done")
        dve_step = sem("dve_step")
        table_done = sem("table_done")
        tern_done = sem("tern_done")
        fq_step = sem("fq_step")
        scores_ready = sem("scores_ready")
        exp_done = sem("exp_done")
        pv_done = sem("pv_done")
        norm_done = sem("norm_done")
        hi_done = sem("hi_done")
        raw_done = sem("raw_done")
        ready = {r: sem(f"ready_{r}") for r in "AM"}
        free = {r: sem(f"free_{r}") for r in "AM"}
        max_done = sem("max_done")
        lnden_done = sem("lnden_done")
        recip_done = sem("recip_done")
        newton_done = sem("newton_done")
        apart = sem("apart")

        block = ctx.enter_context(nc.Block())

        NCONST = 7
        FQ_STEPS = 7
        TURNS = NB // HB
        TURNS0 = KB // HB

        def wait_apart(engine, sem, value):
            engine.wait_ge(sem, value)
            engine.sem_inc(apart, 1)

        def index(i, name):
            return ring_index(i, name, NP)

        def prep_index(i, name):
            if isinstance(i, int) and i == 0:
                return PROLOGUE[ring_of(name)].index(name)
            return index(i - 1, name)

        TAIL = index(NP - 1, LAST["A"][-1]) + 1
        TAIL_BANK = len(LAST["A"]) % 2

        @block.sync
        def _(sp):
            def load_input(b):
                sp.dma_start(x_sb[:, b * KB:(b + 1) * KB, :],
                             x_dram[b, :, :].rearrange("(n p) d -> p n d", p=P)).then_inc(x_landed[b], 16)

            def load_w(i, p):
                for at, w in enumerate((wq_dram, wk_dram, wv_dram)):
                    sp.dma_start(w_in[p][:, at, :], w[:, bass.ds((i % NPB) * P, P)]
                                 ).then_inc(wqkv_landed[p], 16)

            def load_x(i):
                b = (i // NPB) % B
                sp.dma_start(x1_cur[:, :].bitcast(F32), x1T[:, bass.ds(b * S, S)].bitcast(F32)
                             ).then_inc(x_cur_landed, 16)
                sp.dma_start(x2_cur[:, :].bitcast(F32), x2T[:, bass.ds(b * S, S)]
                             ).then_inc(x_cur_landed, 16)

            def load_wo(i):
                sp.dma_start(wo_cur[:, :], wo_dram[bass.ds((i % NPB) * P, P), :]).then_inc(wo_landed, 16)

            def place_maxrow(i, p):
                sp.wait_ge(free["A"], prep_index(i, "T") + 1)
                for h in range(2):
                    sp.dma_start(q1m[p][h][DH:DH + 1, :].bitcast(F32),
                                 maxrow[h * KB:(h + 1) * KB, :].bitcast(F32)).then_inc(maxrow_landed, 16)

            load_input(0)
            load_w(0, 0)
            for b in range(1, B):
                load_input(b)
            load_w(1, 1)
            load_wo(0)
            place_maxrow(0, 0)

            def pair(i, p, first=False, last=False):
                if not last:
                    sp.wait_ge(ready["A"], prep_index(i, "V1") + 1)
                    load_w(i + 2, p)
                if not first:
                    sp.wait_ge(ready["A"], index(i, "Y1p") + 1)
                    load_wo(i)
                if first:
                    sp.wait_ge(x2_rest_done, TURNS - TURNS0)
                if not last:
                    wait_apart(sp, ready["A"], prep_index(i + 1, "K1") + 1)
                    wait_apart(sp, xf_done, 1 if first else i + 1)
                    load_x(i + 2)
                    place_maxrow(i + 1, 1 - p)

            pair(0, 0, first=True)
            with sp.Fori(0, (NP - 2) // 2) as j:
                pair(2 * j + 1, 1)
                pair(2 * j + 2, 0)
            pair(NP - 1, 1, last=True)
            sp.wait_ge(free["A"], index(NP - 1, "D1p") + 1)

            def store(b, n0, n1):
                sp.dma_start(out_dram[b, n0 * P:n1 * P, :].rearrange("(n p) d -> p n d", p=P),
                             x_sb[:, b * KB + n0:b * KB + n1, :]).then_inc(out_stored, 16)

            for b in range(B - 1):
                store(b, 0, KB)
            sp.wait_ge(free["A"], index(NP - 1, "Y0") + 1)
            store(B - 1, 0, HB)
            sp.wait_ge(free["A"], TAIL + 2)
            store(B - 1, HB, KB)
            sp.wait_ge(out_stored, 16 * (B + 1))

        @block.gpsimd
        def _(pool):
            g = nc.gpsimd
            g.memset(ident[:, :], 0.0).then_inc(pool_step, 1)
            g.memset(ident_b[:, :], 0.0).then_inc(pool_step, 1)
            g.memset(causal_b[:, :], 0.0).then_inc(pool_step, 1)
            g.memset(ones[:, :], 1.0).then_inc(consts_done, 1)
            g.memset(big[:, 0, :], 1e4).then_inc(consts_done, 1)
            g.memset(big[:, 1, :], -1e4).then_inc(consts_done, 1)
            g.iota(key_no[:, :], [[P, KB]], base=0, channel_multiplier=1,
                   allow_small_or_imprecise_dtypes=True).then_inc(consts_done, 1)
            pool.wait_ge(pool_step, 3)
            g.affine_select(out=ident[:, :], in_=ident[:, :], compare_op=ALU.not_equal, fill=1.0,
                            base=0, pattern=[[-1, P]], channel_multiplier=1).then_inc(consts_done, 1)
            g.affine_select(out=ident_b[:, :], in_=ident_b[:, :], compare_op=ALU.not_equal, fill=1.0,
                            base=0, pattern=[[-1, P]], channel_multiplier=1).then_inc(consts_done, 1)
            g.affine_select(out=causal_b[:, :], in_=causal_b[:, :], compare_op=ALU.is_ge, fill=MASKED,
                            base=0, pattern=[[-1, P]], channel_multiplier=1).then_inc(consts_done, 1)

            def split_w(i, p):
                wait_apart(pool, wqkv_landed[p], (i - p) * 24 + 48)
                g.tensor_scalar(w1[p][:, :, :], w_in[p][:, 0:2, :], 1.0, None, ALU.mult).then_inc(w_split, 1)
                pool.wait_ge(w_split, i * 2 + 1)
                g.tensor_tensor(w2[p][:, :, :], w_in[p][:, 0:2, :], w1[p][:, :, :].bitcast(F32), ALU.subtract
                                ).then_inc(w_split, 1)

            def whole_x():
                g.tensor_tensor(xf_cur[:, :], x1_cur[:, :].bitcast(F32), x2_cur[:, :].bitcast(F32), ALU.add
                                ).then_inc(xf_done, 1)

            split_w(0, 0)
            split_w(1, 1)
            pool.wait_ge(x2_done, 2 * TURNS0)
            whole_x()

            def pair_table(i, p):
                g.tensor_copy(tab_cur[p][:, :, :, :],
                              table[:, bass.ds(i % NPB, 1), :, :, :].rearrange("p o a k h -> p (o a) k h")
                              ).then_inc(tab_done, 1)

            pool.wait_ge(table_done, 1)
            pair_table(0, 0)

            def add_bias(b):
                pool.wait_ge(xn_done, KB * (b + 1))
                rows = x_sb[:, b * KB:(b + 1) * KB, :]
                g.tensor_tensor(rows, rows, bias_b[:, :].unsqueeze(1).to_broadcast([P, KB, P]), ALU.add
                                ).then_inc(bias_added, 1)

            def feed_forward_block(i):
                g.tensor_tensor(fx[:, :], x1T[:, bass.ds(i * P, P)].bitcast(F32),
                                x2T[:, bass.ds(i * P, P)], ALU.add).then_inc(fx_done, 1)

            pool.wait_ge(small_landed, 48)
            add_bias(0)
            feed_forward_block(0)
            for n in range(TURNS0, TURNS):
                cols = slice(n * HALF, (n + 1) * HALF)
                pool.wait_ge(turned_out, n - TURNS0 + 1)
                g.tensor_tensor(x2T[:, cols].bitcast(F32R), x2T[:, cols], x1T[:, cols].bitcast(F32),
                                ALU.subtract).then_inc(x2_rest_done, 1)

            pool.wait_ge(x2_rest_done, TURNS - TURNS0)

            def pair(i, p, last=False):

                def select(t):
                    lo = first_col(t)
                    wait_apart(pool, exp_done, (i * NT + (t + 1)) * 2)
                    d = prob[t % NPROB][:, :, lo:lo + P]
                    g.affine_select(out=d, in_=d, compare_op=ALU.is_ge, fill=0.0, base=0,
                                    pattern=[[0, 2], [1, P]], channel_multiplier=-1).then_inc(sel_done, 1)

                def add(t):
                    c, kb = TILES[t]
                    lo = first_col(t)
                    pr = prob[t % NPROB]
                    if kb == 0 and not (isinstance(i, int) and i == 0):
                        pool.wait_ge(ready["A"], (index(i - 1, "D0") if c == 0 else index(i, "D1p")) + 1)
                    if t == 0:
                        wait_apart(pool, sel_done, i * NDIAG + 1)
                    elif is_diag(t):
                        pool.wait_ge(sel_done, i * NDIAG + diag_upto[t])
                    else:
                        pool.wait_ge(exp_done, (i * NT + (t + 1)) * 2)
                    if t == HB and not last:
                        split_w(i + 2, p)
                    if isinstance(i, int) and i == 0 and t in (5, 7, 9):
                        add_bias((5, 7, 9).index(t) + 1)
                    acc = psumd[c]
                    if kb == 0:
                        if c == 0:
                            g.tensor_scalar(acc[:, :, 0:P], pr[:, :, 0:P], 1.0, None, ALU.mult)
                    elif kb == 1:
                        g.tensor_tensor(acc[:, :, lo:HALF], prob[(t - 1) % NPROB][:, :, lo:HALF],
                                        pr[:, :, lo:HALF], ALU.add).then_inc(acc_done, 2)
                    else:
                        pool.wait_ge(acc_done, i * NT + t)
                        g.tensor_tensor(acc[:, :, lo:HALF], acc[:, :, lo:HALF], pr[:, :, lo:HALF],
                                        ALU.add).then_inc(acc_done, 1)

                for t in range(NT):
                    if is_diag(t):
                        select(t)
                    if t == 0 and not last:
                        pair_table(i + 1, 1 - p)
                    if t == 7 and not last:
                        pool.wait_ge(fq_step, i * FQ_STEPS + 1)
                        feed_forward_block(i + 1)
                    if t >= 1:
                        add(t - 1)
                    if t == HB and not last and not (isinstance(i, int) and i == 0):
                        pool.wait_ge(x_cur_landed, i * 32)
                        pool.wait_ge(ready["A"], prep_index(i, "V1") + 1)
                        whole_x()
                add(NT - 1)

            pair(0, 0)
            with pool.Fori(0, (NP - 2) // 2) as j:
                pair(2 * j + 1, 1)
                pair(2 * j + 2, 0)
            pair(NP - 1, 1, last=True)

        @block.scalar
        def _(act):
            a = nc.scalar
            act.dma_start(span_b[:, :], span_dram.rearrange("a h b c -> (a b c) h").to_broadcast([P, H])
                          ).then_inc(span_landed, 16)
            for dst, src in ((bias_b[:, :], bias_dram.unsqueeze(0).to_broadcast([P, P])),
                             (scale_b[:, :], scale_dram.to_broadcast([P, 1])),
                             (tern_i[:, :], tern_dram[:, :])):
                act.dma_start(dst, src).then_inc(small_landed, 16)
            a.preload_act_table_set("natural_log_exp_and_others")

            def rstd_start(group, blocks):
                act.wait_ge(var_done, group)
                a.activation(lnv[:, blocks], vpe[:, blocks], ACT.Ln).then_inc(lnv_done, 1)
                act.wait_ge(lnv_done, group)
                a.activation(rs0[:, blocks], lnv[:, blocks], ACT.Exp, scale=-0.5).then_inc(rs0_done, 1)

            rstd_start(1, slice(0, KB))
            for n in range(TURNS0):
                cols = slice(n * HALF, (n + 1) * HALF)
                act.wait_ge(turned_ready, n + 1)
                a.activation(x1_cur[:, cols], scores[:, n % NSCORE, :], ACT.Copy).then_inc(x1_done, 1)
                a.activation(x1T[:, cols], scores[:, n % NSCORE, :], ACT.Copy).then_inc(x1_done, 1)
                if n == 0:
                    act.wait_ge(wgt_done, 1)
                    a.activation(table[:, :, 0, :, :], wgt[:, :, :, :], ACT.Ln).then_inc(ln_done, 1)

            def exps(i, p, t):
                lo = first_col(t)
                if not (isinstance(i, int) and i == 0 and t < NPROB):
                    act.wait_ge(pv_done, i * NT + (t - NPROB + 1))
                    act.wait_ge(acc_done, i * NT + (t - NPROB + 1))
                if t == 0:
                    act.wait_ge(tab_done, i + 1)
                kb = TILES[t][1]
                for h in range(2):
                    act.wait_ge(scores_ready, i * (2 * NT) + (2 * t + h + 1))
                    a.activation(prob[t % NPROB][:, h, lo:HALF], scores[:, (2 * t + h) % NSCORE, lo:HALF],
                                 ACT.Exp, bias=tab_cur[p][:, 0, kb, h:h + 1], scale=1.0 / DH
                                 ).then_inc(exp_done, 1)

            def pv_out(i, c):
                act.wait_ge(pv_done, i * NT + (HB if c == 0 else NT))
                if not (isinstance(i, int) and i == 0):
                    act.wait_ge(norm_done, i * 2 + (c - 1))
                a.activation(pv_raw[c][:, :], pv[:, :], ACT.Copy).then_inc(raw_done, 1)

            def reciprocal(i, c, n, r):
                act.wait_ge(ready["A"], n + 1)
                a.activation(lnden[:, :], rings["A"][:, r, :], ACT.Ln).then_inc(lnden_done, 1)
                act.wait_ge(lnden_done, i * 2 + (c + 1))
                a.activation(rden[0][:, :], lnden[:, :], ACT.Exp, scale=-1.0).then_inc(recip_done, 1)

            def high_parts(i, p, name, r):
                act.wait_ge(ready["A"], prep_index(i, name) + 1)
                cols = slice(int(name[1]) * HALF, (int(name[1]) + 1) * HALF)
                for h in range(2):
                    src = rings["A"][h * DH:(h + 1) * DH, r, :]
                    if name[0] == "Q":
                        a.activation(q1m[p][h][0:DH, cols], src, ACT.Copy)
                        a.activation(q12[p][h][0:DH, cols], src, ACT.Copy).then_inc(hi_done, 1)
                    else:
                        a.activation(k11[p][h][0:DH, cols], src, ACT.Copy)
                        a.activation(k11[p][h][DH:P, cols], src, ACT.Copy).then_inc(hi_done, 1)

            def turned(n):
                cols = slice(n * HALF, (n + 1) * HALF)
                act.wait_ge(turned_ready, n + 1)
                a.activation(x1T[:, cols], scores[:, n % NSCORE, :], ACT.Copy)
                a.activation(x2T[:, cols], scores[:, n % NSCORE, :], ACT.Copy).then_inc(turned_out, 1)

            for u in PE_PROLOGUE:
                if u[0] == "X" and int(u[1:]) >= TURNS0:
                    turned(int(u[1:]))
                elif u[0] in "QK":
                    high_parts(0, 0, u, bank(u, PROLOGUE))
                    if u == "Q1":
                        rstd_start(2, slice(KB, NB))

            def pair(i, p, where=STEADY):
                for u in kept(ACT_PLAN, where is FIRST, where is LAST):
                    if u[0] == "e":
                        exps(i, p, int(u[1:]))
                    elif u == "P1p":
                        pv_out(i - 1, 1)
                    elif u == "P0":
                        pv_out(i, 0)
                    elif u == "D0":
                        reciprocal(i, 0, index(i, u), bank(u, where))
                    elif u == "D1p":
                        reciprocal(i - 1, 1, index(i, u), bank(u, where))
                    else:
                        high_parts(i + 1, 1 - p, u, bank(u, where))

            pair(0, 0, FIRST)
            with act.Fori(0, (NP - 2) // 2) as j:
                pair(2 * j + 1, 1)
                pair(2 * j + 2, 0)
            pair(NP - 1, 1, LAST)
            pv_out(NP - 1, 1)
            reciprocal(NP - 1, 1, TAIL, TAIL_BANK)

        @block.vector
        def _(dve):
            v = nc.vector
            steps = [0]

            def then(ins):
                steps[0] += 1
                ins.then_inc(dve_step, 1)
                dve.wait_ge(dve_step, steps[0])

            def statistics(b):
                dve.wait_ge(x_landed[b], 16)
                for n in range(b * KB, (b + 1) * KB):
                    last = v.bn_stats(stats[:, n, :], x_sb[:, n, :])
                then(last)

            def variances(n0, n1):
                for n in range(n0, n1):
                    last = v.bn_aggr(mv[:, n, :], stats[:, n, :])
                then(last)
                v.tensor_scalar(vpe[:, n0:n1], mv[:, n0:n1, 1], EPS_LN, None, ALU.add).then_inc(var_done, 1)

            def rstd_finish(group, bl):
                dve.wait_ge(rs0_done, group)
                then(v.tensor_tensor(tmp[:, bl], rs0[:, bl], rs0[:, bl], ALU.mult))
                then(v.tensor_tensor(tmp[:, bl], tmp[:, bl], vpe[:, bl], ALU.mult))
                then(v.tensor_scalar(tmp[:, bl], tmp[:, bl], -0.5, 1.5, ALU.mult, ALU.add))
                v.tensor_tensor(rstd[:, bl], rs0[:, bl], tmp[:, bl], ALU.mult).then_inc(rstd_done, 1)
                dve.wait_ge(rstd_done, group)

            def normalise(b):
                for n in range(b * KB, (b + 1) * KB):
                    v.tensor_scalar(xn_sb[:, n * P:(n + 1) * P], x_sb[:, n, :], mv[:, n, 0:1],
                                    rstd[:, n:n + 1], ALU.subtract, ALU.mult).then_inc(xn_done, 1)

            for p in range(2):
                for h in range(2):
                    v.memset(k2n[p][h][DH:DH + 1, :].bitcast(F32), -1.0).then_inc(minus_ones_done, 1)
            statistics(0)
            variances(0, KB)
            rstd_finish(1, slice(0, KB))
            normalise(0)
            dve.wait_ge(consts_done, NCONST)
            dve.wait_ge(span_landed, 16)
            then(v.tensor_scalar(span_b[:, :], span_b[:, :], float(S), None, ALU.mult))
            for h in range(H):
                last = v.tensor_scalar(mask[:, h // 2, :, h % 2], key_no[:, :], span_b[:, h:h + 1],
                                       1.0 / (RAMP + 1), ALU.add, ALU.mult)
            then(last)
            then(v.tensor_scalar(mask[:, :, :, :], mask[:, :, :, :], 0.0, 1.0, ALU.max, ALU.min))
            v.tensor_scalar(wgt[:, :, :, :], mask[:, :, :, :], EPS_SUM, None, ALU.add).then_inc(wgt_done, 1)
            for n in range(TURNS0):
                cols = slice(n * HALF, (n + 1) * HALF)
                dve.wait_ge(x1_done, 2 * n + 2)
                for x2, x1 in ((x2_cur[:, cols], x1_cur), (x2T[:, cols].bitcast(F32R), x1T)):
                    v.tensor_tensor(x2, scores[:, n % NSCORE, :], x1[:, cols].bitcast(F32), ALU.subtract
                                    ).then_inc(x2_done, 1)
            dve.wait_ge(wgt_done, 1)
            then(v.reciprocal(wrec[:, :, :, :], wgt[:, :, :, :]))
            dve.wait_ge(ln_done, 1)
            v.tensor_tensor(table[:, :, 1, :, :], mask[:, :, :, :], wrec[:, :, :, :],
                            ALU.mult).then_inc(table_done, 1)
            def quantisation_scale():
                dve.wait_ge(small_landed, 48)
                then(v.tensor_scalar(sc[:, 0:1], scale_b[:, :], 1e-5, None, ALU.max))
                v.memset(sc[:, 2:3], 0.0)
                v.memset(sc[:, 3:4], 1.0)
                then(v.tensor_scalar(sc[:, 4:5].bitcast(U32), scale_b[:, :], FLT_MAX, None, ALU.is_le))
                v.copy_predicated(sc[:, 2:3], sc[:, 4:5].bitcast(U32), sc[:, 0:1])
                then(v.copy_predicated(sc[:, 3:4], sc[:, 4:5].bitcast(U32), sc[:, 0:1]))
                then(v.reciprocal(sc[:, 5:6], sc[:, 3:4]))
                v.tensor_scalar(tern[:, :], tern_i[:, :], -1.0, None, ALU.add).then_inc(tern_done, 1)

            def low_parts(i, p, name, r):
                before = i * 8 + 2 * [u for u in of_prep(DVE_PLAN) if u[0] in "QK"].index(name)
                cols = slice(int(name[1]) * HALF, (int(name[1]) + 1) * HALF)
                for h in range(2):
                    src = rings["A"][h * DH:(h + 1) * DH, r, :]
                    dve.wait_ge(hi_done, before + (h + 1))
                    if name[0] == "Q":
                        last = v.tensor_tensor(q12[p][h][DH:P, cols], src,
                                               q1m[p][h][0:DH, cols].bitcast(F32), ALU.subtract)
                    else:
                        last = v.tensor_tensor(k2n[p][h][0:DH, cols], src,
                                               k11[p][h][0:DH, cols].bitcast(F32), ALU.subtract)
                last.then_inc(free["A"], 1)

            def prep_unit(i, p, name, r):
                if name[0] in "QK":
                    low_parts(i, p, name, r)
                    return
                dve.wait_ge(ready[ring_of(name)], prep_index(i, name) + 1)
                if name[0] == "M":
                    j, k0, n, heads = MAX_UNITS[int(name[1:])]
                    dst = rowmax[p][:, :, j] if k0 == 0 else rowmax2[p][:, :, j - HB]
                    v.tensor_reduce(dst[:, heads[0]:heads[-1] + 1],
                                    rings["M"][:, r, 0:n * len(heads)].rearrange("p (h k) -> p h k", k=n),
                                    axis=AX, op=ALU.max).then_inc(free["M"], 1)
                    if name == M[-1]:
                        dve.wait_ge(free["M"], prep_index(i, name) + 1)
                        v.tensor_tensor(rowmax[p][:, :, HB:KB], rowmax[p][:, :, HB:KB],
                                        rowmax2[p][:, :, :], ALU.max).then_inc(max_done, 1)
                elif name == "T":
                    v.tensor_copy(maxrow[:, :], rings["A"][0:2 * KB, r, 0:P]).then_inc(free["A"], 1)
                else:
                    if name == "V0":
                        dve.wait_ge(tab_done, i + 1)
                    b0 = HB * int(name[1])
                    v.tensor_tensor(v_sb[p][:, b0:b0 + HB, :, :],
                                    rings["A"][:, r, :].rearrange("p (k h d) -> p k h d", k=HB, h=2),
                                    tab_cur[p][:, 1, b0:b0 + HB, :].unsqueeze(3).to_broadcast([P, HB, 2, DH]),
                                    ALU.mult).then_inc(free["A"], 1)

            for u in DVE_PROLOGUE:
                if u[0] == "S":
                    statistics(int(u[1:]))
                    if int(u[1:]) == B - 1:
                        variances(KB, NB)
                        quantisation_scale()
                elif u == "R":
                    rstd_finish(2, slice(KB, NB))
                elif u[0] == "N":
                    normalise(int(u[1:]))
                else:
                    prep_unit(0, 0, u, bank(u, PROLOGUE))
            dve.wait_ge(ready["A"], len(PROLOGUE["A"]))
            v.tensor_copy(ternT[:, :], rings["A"][:, bank("W", PROLOGUE), 0:P]).then_inc(free["A"], 1)
            def quantise(i, step):
                if step > FQ_STEPS - 2:
                    wait_apart(dve, fq_step, i * FQ_STEPS + (step - 1))
                elif step > 1:
                    dve.wait_ge(fq_step, i * FQ_STEPS + (step - 1))
                else:
                    dve.wait_ge(fx_done, i + 1)
                if step == 1:
                    ins = v.tensor_scalar(fq[:, :], fx[:, :], sc[:, 5:6], ACT_QB, ALU.mult, ALU.min)
                elif step == 2:
                    ins = v.tensor_scalar(fq[:, :], fq[:, :], -ACT_QB, ROUND, ALU.max, ALU.add)
                elif step == 3:
                    ins = v.tensor_scalar(fq[:, :], fq[:, :], -ROUND, sc[:, 2:3], ALU.add, ALU.mult)
                elif step == 4:
                    ins = v.tensor_scalar(over[:, 0, :], fq[:, :], FLT_MAX, None, ALU.is_gt)
                elif step == 5:
                    ins = v.tensor_scalar(over[:, 1, :], fq[:, :], -FLT_MAX, None, ALU.is_lt)
                elif step == 6:
                    ins = v.copy_predicated(fq[:, :], over[:, 0, :], big[:, 0, :])
                else:
                    ins = v.copy_predicated(fq[:, :], over[:, 1, :], big[:, 1, :])
                ins.then_inc(fq_step, 1)

            def normalise_pv(i, c, n, r):
                dve.wait_ge(recip_done, i * 2 + (c + 1))
                v.tensor_tensor(rden[1][:, :], rings["A"][:, r, :], rden[0][:, :], ALU.mult
                                ).then_inc(free["A"], 1)
                dve.wait_ge(free["A"], n + 1)
                v.scalar_tensor_tensor(out=rden[2][:, :], in0=rden[1][:, :], scalar=2.0, in1=rden[0][:, :],
                                       op0=ALU.subtract, op1=ALU.mult).then_inc(newton_done, 1)
                dve.wait_ge(newton_done, i * 2 + (c + 1))
                dve.wait_ge(raw_done, i * 2 + (c + 1))
                v.scalar_tensor_tensor(out=o_sb[c][:, :], in0=pv_raw[c][:, :], scalar=-1.0,
                                       in1=rden[2][:, :], op0=ALU.mult, op1=ALU.mult).then_inc(norm_done, 1)

            def add_output(i, c, n, r):
                dve.wait_ge(ready["A"], n + 1)
                rows = x_sb[:, bass.ds((i // NPB) * KB + c * HB, HB), :]
                v.tensor_tensor(rows, rows, rings["A"][:, r, :].rearrange("p (n d) -> p n d", n=HB),
                                ALU.add).then_inc(free["A"], 1)

            def pair(i, p, where=STEADY):
                bias_waited = where is not FIRST
                for u in kept(DVE_PLAN, where is FIRST, where is LAST):
                    if u[0] == "q":
                        quantise(i, int(u[1:]))
                        continue
                    if u[0] in "FY" and not bias_waited:
                        dve.wait_ge(bias_added, 1)
                        bias_waited = True
                    r = bank(u, where)
                    if u == "D0":
                        normalise_pv(i, 0, index(i, u), r)
                    elif u == "D1p":
                        normalise_pv(i - 1, 1, index(i, u), r)
                    elif u == "Y0":
                        add_output(i, 0, index(i, u), r)
                    elif u == "Y1p":
                        add_output(i - 1, 1, index(i, u), r)
                    elif u == "F":
                        dve.wait_ge(ready["A"], index(i, u) + 1)
                        rows = x_sb[:, bass.ds(i, 1), :]
                        v.tensor_tensor(rows, rows, rings["A"][:, r, 0:P].unsqueeze(1), ALU.add
                                        ).then_inc(free["A"], 1)
                    else:
                        prep_unit(i + 1, 1 - p, u, r)

            pair(0, 0, FIRST)
            dve.wait_ge(bias_added, B)
            with dve.Fori(0, (NP - 2) // 2) as j:
                pair(2 * j + 1, 1)
                pair(2 * j + 2, 0)
            pair(NP - 1, 1, LAST)
            normalise_pv(NP - 1, 1, TAIL, TAIL_BANK)
            add_output(NP - 1, 1, TAIL + 1, 1 - TAIL_BANK)

        @block.tensor
        def _(pe):
            t_ = nc.tensor
            pe.wait_ge(consts_done, NCONST)

            def begin_unit(ring, n):
                if not isinstance(n, int) or n >= 2:
                    pe.wait_ge(free[ring], n - 1)

            def bank_left(n):
                if n < TURNS0:
                    pe.wait_ge(x2_done, 2 * n + 2)
                else:
                    pe.wait_ge(turned_out, n - TURNS0 + 1)

            def turn(n):
                if n >= NSCORE:
                    bank_left(n - NSCORE)
                pe.wait_ge(xn_done, HB * (n + 1))
                for k in range(HB):
                    block = n * HB + k
                    last = t_.transpose(scores[:, n % NSCORE, k * P:(k + 1) * P],
                                        xn_sb[:, block * P:(block + 1) * P], ident[:, :])
                last.then_inc(turned_ready, 1)

            def prep_unit(i, p, name, r):
                ring = rings[ring_of(name)]
                begin_unit(ring_of(name), prep_index(i, name))
                if name == "Q0":
                    pe.wait_ge(w_split, i * 2 + 2)
                    if not (isinstance(i, int) and i < 2):
                        pe.wait_ge(x_cur_landed, (i - 1) * 32)
                if isinstance(i, int) and i == 0 and name in ("Q0", "Q1", "V1"):
                    pe.wait_ge(x2_done, 1 if name == "Q0" else 3)
                parts = ((w1, x1_cur), (w1, x2_cur), (w2, x1_cur))
                if name[0] in "QK":
                    c = int(name[1])
                    for at, (w, x) in enumerate(parts):
                        last = t_.matmul(ring[:, r, :], w[p][:, "QK".index(name[0]), :],
                                         x[:, c * HALF:(c + 1) * HALF], start=(at == 0), stop=(at == 2))
                elif name[0] == "V":
                    if name == "V0":
                        pe.wait_ge(xf_done, 1 if isinstance(i, int) and i < 2 else i)
                    for k in range(HB):
                        kb = HB * int(name[1]) + k
                        last = t_.matmul(ring[:, r, k * P:(k + 1) * P], xf_cur[:, kb * P:(kb + 1) * P],
                                         w_in[p][:, 2, :], start=True, stop=True)
                elif name[0] == "M":
                    need = {M[0]: "K0", M[6]: "Q1", M[14]: "K1"}.get(name)
                    if need:
                        pe.wait_ge(free["A"], prep_index(i, need) + 1)
                    j, k0, w, heads = MAX_UNITS[int(name[1:])]
                    for at, h in enumerate(heads):
                        out = ring[:, r, at * w:(at + 1) * w]
                        diag = k0 + w == (j + 1) * P
                        last = t_.matmul(out, q12[p][h][:, j * P:(j + 1) * P], k11[p][h][:, k0:k0 + w],
                                         start=True, stop=not diag)
                        if diag:
                            last = t_.matmul(ring[:, r, (at + 1) * w - P:(at + 1) * w], ident_b[:, :],
                                             causal_b[:, :], start=False, stop=True)
                else:
                    pe.wait_ge(max_done, i + 1)
                    last = t_.matmul(ring[0:2 * KB, r, 0:P], rowmax[p][:, :, :].rearrange("p h j -> p (h j)"),
                                     ident[:, :], start=True, stop=True)
                last.then_inc(ready[ring_of(name)], 1)

            for u in PE_PROLOGUE[:-1]:
                if u[0] == "X":
                    turn(int(u[1:]))
                else:
                    prep_unit(0, 0, u, bank(u, PROLOGUE))
            for n in range(TURNS - NSCORE, TURNS):
                bank_left(n)
            pe.wait_ge(minus_ones_done, 4)
            begin_unit("A", PROLOGUE["A"].index("W"))
            pe.wait_ge(tern_done, 1)
            t_.transpose(rings["A"][:, bank("W", PROLOGUE), 0:P], tern[:, :], ident[:, :]
                         ).then_inc(ready["A"], 1)

            def denominators(i, c, r):
                pe.wait_ge(acc_done, i * NT + (HB if c == 0 else NT))
                for h in range(2):
                    last = t_.matmul(rings["A"][h * DH:(h + 1) * DH, r, :], ones[:, :], psumd[c][:, h, :],
                                     start=True, stop=True)
                last.then_inc(ready["A"], 1)

            def output_projection(i, c, r):
                pe.wait_ge(norm_done, i * 2 + (c + 1))
                pe.wait_ge(wo_landed, (i + 1) * 16)
                for k in range(HB):
                    last = t_.matmul(rings["A"][:, r, k * P:(k + 1) * P], o_sb[c][:, k * P:(k + 1) * P],
                                     wo_cur[:, :], start=True, stop=True)
                last.then_inc(ready["A"], 1)

            def own_unit(i, name, r):
                begin_unit("A", index(i, name))
                if name == "D0":
                    denominators(i, 0, r)
                elif name == "D1p":
                    denominators(i - 1, 1, r)
                elif name == "Y0":
                    output_projection(i, 0, r)
                elif name == "Y1p":
                    output_projection(i - 1, 1, r)
                else:
                    pe.wait_ge(fq_step, (i + 1) * FQ_STEPS)
                    t_.matmul(rings["A"][:, r, 0:P], fq[:, :], ternT[:, :], start=True, stop=True
                              ).then_inc(ready["A"], 1)

            def scores_of(i, p, t, h):
                c, kb = TILES[t]
                lo = first_col(t)
                cols = slice(c * HALF + lo, (c + 1) * HALF)
                n = 2 * t + h
                if not (isinstance(i, int) and i == 0 and n < NSCORE):
                    pe.wait_ge(exp_done, i * (2 * NT) + (n - NSCORE + 1))
                if t == 0 and h == 0:
                    pe.wait_ge(maxrow_landed, (i + 1) * 32)
                out = scores[:, n % NSCORE, lo:HALF]
                keys = slice(kb * P, (kb + 1) * P)
                t_.matmul(out, k11[p][h][:, keys], q12[p][h][:, cols], start=True, stop=False)
                t_.matmul(out, k2n[p][h][:, keys], q1m[p][h][:, cols], start=False, stop=True
                          ).then_inc(scores_ready, 1)

            def pv_of(i, p, t):
                c, kb = TILES[t]
                lo = first_col(t)
                if is_diag(t):
                    pe.wait_ge(sel_done, i * NDIAG + diag_upto[t])
                else:
                    pe.wait_ge(exp_done, i * (2 * NT) + 2 * (t + 1))
                if kb == 0 and not (isinstance(i, int) and i == 0 and c == 0):
                    pe.wait_ge(raw_done, i * 2 + c)
                if t == 0:
                    pe.wait_ge(free["A"], prep_index(i, "V1") + 1)
                for h in range(2):
                    last = t_.matmul(pv[h * DH:(h + 1) * DH, lo:HALF], v_sb[p][:, kb, h, :],
                                     prob[t % NPROB][:, h, lo:HALF], start=(kb == 0),
                                     stop=(kb == HB * (c + 1) - 1))
                last.then_inc(pv_done, 1)

            def pair(i, p, where=STEADY):
                for u in kept(PE_LEAD, where is FIRST, where is LAST):
                    prep_unit(i + 1, 1 - p, u, bank(u, where))
                scores_of(i, p, 0, 0)
                scores_of(i, p, 0, 1)
                for s in range(NT):
                    for place in range(3):
                        if place == 2:
                            pv_of(i, p, s)
                        elif s + 1 < NT:
                            scores_of(i, p, s + 1, place)
                        for u in kept(PE_PLAN[s][place], where is FIRST, where is LAST):
                            if u in OF_THIS_PAIR or u in OF_PAIR_BEFORE:
                                own_unit(i, u, bank(u, where))
                            else:
                                prep_unit(i + 1, 1 - p, u, bank(u, where))

            pair(0, 0, FIRST)
            with pe.Fori(0, (NP - 2) // 2) as j:
                pair(2 * j + 1, 1)
                pair(2 * j + 2, 0)
            pair(NP - 1, 1, LAST)
            begin_unit("A", TAIL)
            denominators(NP - 1, 1, TAIL_BANK)
            begin_unit("A", TAIL + 1)
            output_projection(NP - 1, 1, 1 - TAIL_BANK)


_INS = ["L0_attn_query", "L0_attn_Wq", "L0_attn_Wk", "L0_attn_Wv", "L0_attn_Wo", "L0_attn_span_val",
        "L0_ffn_ternary_weight", "L0_ffn_bias", "L0_ffn_act_scale"]


def kernel(**inputs):
    import concourse.bacc as bacc
    import numpy as np
    from concourse.bass_utils import run_bass_kernel_spmd

    nc = bacc.Bacc("TRN2", target_bir_lowering=False, num_devices=1)
    arrays, args = {}, []
    for name in _INS:
        a = np.ascontiguousarray(inputs[name])
        if a.ndim == 0:
            a = a.reshape(1, 1)
        arrays[f"in_{name}"] = a
        args.append(nc.dram_tensor(f"in_{name}", a.shape, mybir.dt.from_np(a.dtype), kind="ExternalInput").ap())
    shape = inputs["L0_attn_query"].shape
    args.append(nc.dram_tensor("out_0", shape, F32, kind="ExternalOutput").ap())
    attention_ffn(nc, *args)
    r = run_bass_kernel_spmd(nc, [arrays], core_ids=[0])
    return r.results[0]["out_0"]
```
